# Optimizing a Trainium2 kernel written in Bass

```python
import numpy as np
import jax
import jax.numpy as jnp

def _softmax(x, axis=-1):
    return jax.nn.softmax(x, axis=axis)

def _gelu(x):
    return jax.nn.gelu(x, approximate=True)

def _silu(x):
    return jax.nn.silu(x)

def _sigmoid(x):
    return jax.nn.sigmoid(x)

def _layernorm(x, axis=-1, eps=1e-05):
    m = jnp.mean(x, axis=axis, keepdims=True)
    v = jnp.var(x, axis=axis, keepdims=True)
    return (x - m) / jnp.sqrt(v + eps)

def _scatter_add(tgt, idx, src, axis=0):
    return tgt.at[idx].add(src)

def _segment_sum(src, seg, n):
    return jax.ops.segment_sum(src, seg, n)
kernel_name = 'mk_seq_preln_d1_jaxref_r8_a54337'

def setup_inputs(seed: int=0):
    np.random.seed(seed)
    _w = jnp.asarray

    def _L0_attn_setup():
        import jax, jax.numpy as jnp
        import numpy as np
        DEPTH = 2
        DIM = 128
        SDIM = 32
        B = 32
        S = 64
        EPS = 1e-05

        def _run_selective_scan(x, Wd, bd, Wi, bi, A_log, Wo, bo):
            delta = jax.nn.softplus(jnp.einsum('bsd,dn->bsn', x, Wd) + bd)
            u = jnp.einsum('bsd,dn->bsn', x, Wi) + bi
            decay = jnp.exp(-delta * jax.nn.softplus(A_log))
            drive = delta * u

            def step(h, t):
                d, g = t
                h = d * h + g
                return (h, h)
            h0 = jnp.zeros((x.shape[0], Wd.shape[1]), x.dtype)
            final, hs = jax.lax.scan(step, h0, (decay.swapaxes(0, 1), drive.swapaxes(0, 1)))
            hs = hs.swapaxes(0, 1)
            y = jnp.einsum('bsn,nd->bsd', hs, Wo) + bo
            return (y, final)

        def _reference_tuple_inner(shot_embeddings, Wd, bd, Wi, bi, A_log, Wo, bo, Ws, bs, gamma, beta):
            hidden = shot_embeddings
            class_state = None
            for l in range(Wd.shape[0]):
                hidden, state = _run_selective_scan(hidden, Wd[l], bd[l], Wi[l], bi[l], A_log[l], Wo[l], bo[l])
                class_state = jnp.einsum('bn,nd->bd', state, Ws[l]) + bs[l]
                hidden = hidden + class_state[:, None, :]
            pooled = class_state + hidden.mean(axis=1)
            mu = pooled.mean(axis=-1, keepdims=True)
            var = pooled.var(axis=-1, keepdims=True)
            class_repr = (pooled - mu) / jnp.sqrt(var + EPS) * gamma + beta
            return (class_repr, hidden)
        key = jax.random.key(seed)
        ks = jax.random.split(key, 10)
        sc = 0.02
        return {'shot_embeddings': jax.random.normal(ks[0], (B, S, DIM), jnp.float32), 'Wd': jax.random.normal(ks[1], (DEPTH, DIM, SDIM), jnp.float32) * sc, 'bd': jnp.zeros((DEPTH, SDIM), jnp.float32), 'Wi': jax.random.normal(ks[2], (DEPTH, DIM, SDIM), jnp.float32) * sc, 'bi': jnp.zeros((DEPTH, SDIM), jnp.float32), 'A_log': jax.random.normal(ks[3], (DEPTH, SDIM), jnp.float32), 'Wo': jax.random.normal(ks[4], (DEPTH, SDIM, DIM), jnp.float32) * sc, 'bo': jnp.zeros((DEPTH, DIM), jnp.float32), 'Ws': jax.random.normal(ks[5], (DEPTH, SDIM, DIM), jnp.float32) * sc, 'bs': jnp.zeros((DEPTH, DIM), jnp.float32), 'gamma': jnp.ones((DIM,), jnp.float32), 'beta': jnp.zeros((DIM,), jnp.float32)}
    _L0_attn_in = _L0_attn_setup()

    def _L0_ffn_setup():
        import jax, jax.numpy as jnp
        import numpy as np
        B, S, D, O, E, K = (2, 256, 128, 128, 8, 2)
        key = jax.random.key(seed)
        ks = jax.random.split(key, 6)

        def w(k, shape, fan_in):
            return jax.random.normal(k, shape, jnp.float32) * fan_in ** (-0.5)
        return {'x': jax.random.normal(ks[0], (B, S, D), jnp.float32), 'gate_w': w(ks[1], (E, D), D), 'gate_b': jnp.zeros((E,), jnp.float32), 'w1': w(ks[2], (E, D, O), D), 'b1': jnp.zeros((E, O), jnp.float32), 'w2': w(ks[3], (E, O, O), O), 'b2': jnp.zeros((E, O), jnp.float32), 'w3': w(ks[4], (E, O, O), O), 'b3': jnp.zeros((E, O), jnp.float32)}
    _L0_ffn_in = _L0_ffn_setup()
    _d = {'L0_attn_shot_embeddings': _L0_attn_in['shot_embeddings'], 'L0_attn_Wd': _L0_attn_in['Wd'], 'L0_attn_bd': _L0_attn_in['bd'], 'L0_attn_Wi': _L0_attn_in['Wi'], 'L0_attn_bi': _L0_attn_in['bi'], 'L0_attn_A_log': _L0_attn_in['A_log'], 'L0_attn_Wo': _L0_attn_in['Wo'], 'L0_attn_bo': _L0_attn_in['bo'], 'L0_attn_Ws': _L0_attn_in['Ws'], 'L0_attn_bs': _L0_attn_in['bs'], 'L0_attn_gamma': _L0_attn_in['gamma'], 'L0_attn_beta': _L0_attn_in['beta'], 'L0_ffn_gate_w': _L0_ffn_in['gate_w'], 'L0_ffn_gate_b': _L0_ffn_in['gate_b'], 'L0_ffn_w1': _L0_ffn_in['w1'], 'L0_ffn_b1': _L0_ffn_in['b1'], 'L0_ffn_w2': _L0_ffn_in['w2'], 'L0_ffn_b2': _L0_ffn_in['b2'], 'L0_ffn_w3': _L0_ffn_in['w3'], 'L0_ffn_b3': _L0_ffn_in['b3']}
    _x0 = _d['L0_attn_shot_embeddings']
    _d['L0_attn_shot_embeddings'] = jax.random.normal(jax.random.fold_in(jax.random.key(seed), 1), (4, 512, 128), dtype=_x0.dtype)
    del _x0
    return _d

def reference(L0_attn_shot_embeddings, L0_attn_Wd, L0_attn_bd, L0_attn_Wi, L0_attn_bi, L0_attn_A_log, L0_attn_Wo, L0_attn_bo, L0_attn_Ws, L0_attn_bs, L0_attn_gamma, L0_attn_beta, L0_ffn_gate_w, L0_ffn_gate_b, L0_ffn_w1, L0_ffn_b1, L0_ffn_w2, L0_ffn_b2, L0_ffn_w3, L0_ffn_b3):

    def _L0_attn_ref(shot_embeddings, Wd, bd, Wi, bi, A_log, Wo, bo, Ws, bs, gamma, beta):
        import jax, jax.numpy as jnp
        import numpy as np
        DEPTH = 2
        DIM = 128
        SDIM = 32
        B = 32
        S = 64
        EPS = 1e-05

        def _run_selective_scan(x, Wd, bd, Wi, bi, A_log, Wo, bo):
            delta = jax.nn.softplus(jnp.einsum('bsd,dn->bsn', x, Wd) + bd)
            u = jnp.einsum('bsd,dn->bsn', x, Wi) + bi
            decay = jnp.exp(-delta * jax.nn.softplus(A_log))
            drive = delta * u

            def step(h, t):
                d, g = t
                h = d * h + g
                return (h, h)
            h0 = jnp.zeros((x.shape[0], Wd.shape[1]), x.dtype)
            final, hs = jax.lax.scan(step, h0, (decay.swapaxes(0, 1), drive.swapaxes(0, 1)))
            hs = hs.swapaxes(0, 1)
            y = jnp.einsum('bsn,nd->bsd', hs, Wo) + bo
            return (y, final)

        def _reference_tuple_inner(shot_embeddings, Wd, bd, Wi, bi, A_log, Wo, bo, Ws, bs, gamma, beta):
            hidden = shot_embeddings
            class_state = None
            for l in range(Wd.shape[0]):
                hidden, state = _run_selective_scan(hidden, Wd[l], bd[l], Wi[l], bi[l], A_log[l], Wo[l], bo[l])
                class_state = jnp.einsum('bn,nd->bd', state, Ws[l]) + bs[l]
                hidden = hidden + class_state[:, None, :]
            pooled = class_state + hidden.mean(axis=1)
            mu = pooled.mean(axis=-1, keepdims=True)
            var = pooled.var(axis=-1, keepdims=True)
            class_repr = (pooled - mu) / jnp.sqrt(var + EPS) * gamma + beta
            return (class_repr, hidden)
        return _reference_tuple_inner(shot_embeddings, Wd, bd, Wi, bi, A_log, Wo, bo, Ws, bs, gamma, beta)[1]

    def _L0_ffn_ref(x, gate_w, gate_b, w1, b1, w2, b2, w3, b3):
        import jax, jax.numpy as jnp
        import numpy as np
        B, S, D, O, E, K = (2, 256, 128, 128, 8, 2)
        probs = jax.nn.softmax(x @ gate_w.T + gate_b, axis=-1)
        _, topi = jax.lax.top_k(probs, K)
        onehot = jax.nn.one_hot(topi, E, dtype=probs.dtype)
        cw = jnp.einsum('bske,bsk->bse', onehot, probs[..., :K])
        out = jnp.zeros(x.shape[:2] + (O,), x.dtype)
        for e in range(E):
            h = jax.nn.relu(x @ w1[e] + b1[e])
            h = jax.nn.relu(h @ w2[e] + b2[e])
            h = h @ w3[e] + b3[e]
            out = out + cw[..., e:e + 1] * h
        return out
    x = L0_attn_shot_embeddings
    x = x + _L0_attn_ref(_layernorm(x, axis=-1), L0_attn_Wd, L0_attn_bd, L0_attn_Wi, L0_attn_bi, L0_attn_A_log, L0_attn_Wo, L0_attn_bo, L0_attn_Ws, L0_attn_bs, L0_attn_gamma, L0_attn_beta)
    x = x + _L0_ffn_ref(_layernorm(x, axis=-1), L0_ffn_gate_w, L0_ffn_gate_b, L0_ffn_w1, L0_ffn_b1, L0_ffn_w2, L0_ffn_b2, L0_ffn_w3, L0_ffn_b3)
    return x

_drawn_inputs = setup_inputs


def setup_inputs(seed=0):
    import zlib

    import numpy as np

    out = dict(_drawn_inputs(seed))
    spreads = {'L0_attn_bd': (0.0, 2.0),
     'L0_attn_bi': (0.0, 0.1),
     'L0_attn_bo': (0.0, 0.1),
     'L0_attn_bs': (0.0, 0.1),
     'L0_attn_gamma': (1.0, 0.2),
     'L0_attn_beta': (0.0, 0.1),
     'L0_ffn_gate_b': (0.0, 0.1),
     'L0_ffn_b1': (0.0, 0.744),
     'L0_ffn_b2': (0.0, 0.517),
     'L0_ffn_b3': (0.0, 0.353)}
    factors = {'L0_attn_Wd': 30.323}
    for name, (base, spread) in spreads.items():
        noise = np.random.default_rng([zlib.crc32(name.encode()), seed]).standard_normal(out[name].shape)
        drawn = base * np.exp(spread * noise) if base else spread * noise
        out[name] = jnp.asarray(drawn.astype(out[name].dtype))
    for name, factor in factors.items():
        out[name] = (out[name] * factor).astype(out[name].dtype)
    return out
```

```python
from contextlib import ExitStack

import concourse.bass as bass
from concourse import mybir

F32 = mybir.dt.float32
F16 = mybir.dt.float16
ALU = mybir.AluOpType
ACT = mybir.ActivationFunctionType
AX = mybir.AxisListType

P = 128
B, S, D = 4, 512, 128
N = 32
L = 2
E = 8
J = S // P
ITEMS = J * E
EPS = 1e-5
FAR = -1e30

R_B1, R_B2, R_GW, R_BO, R_BS, R_BD, R_BI, R_A = 0, E, 2 * E, 3 * E, 3 * E + L, 3 * E + 2 * L, 3 * E + 3 * L, 3 * E + 4 * L
ROWS = 3 * E + 5 * L


def program(nc, x_in, Wd, bd, Wi, bi, A_log, Wo, bo, Ws, bs, gate_w, gate_b, w1, b1, w2, b2, w3, b3, out):
    with ExitStack() as ctx:
        def sb(name, shape, dt=F32):
            return ctx.enter_context(nc.sbuf_tensor(name, shape, dt))

        def sem(name):
            return ctx.enter_context(nc.semaphore(name))

        bank = [ctx.enter_context(nc.psum_tensor(f"bank{i}", [P, 512], F32)) for i in range(8)]
        ZD, ZI = bank[0], bank[1]
        TR1 = bank[2:6]
        PROJ = bank[2:6]
        MISC, CROW = bank[6], bank[6]
        COMP = bank[7]
        TR2 = bank[6:8]
        GATE, CWT, B3P = bank[4], bank[5], bank[6:8]
        Z1, Z2, Y = bank[0:2], bank[2:4], bank[4:6]

        ident = sb("ident", [P, P])
        blocks = sb("blocks", [P, P])
        ones = sb("ones", [L, P])
        eps = sb("eps", [P, 1])
        first = sb("first", [P, E])
        rows = sb("rows", [ROWS, P])
        cols = sb("cols", [P, ROWS])
        wdi = sb("wdi", [P, L, 2, N])
        wos0 = sb("wos0", [2 * N, D])
        wosT = sb("wosT", [P, 2, B, N])
        wdi1 = sb("wdi1", [P, 2, B, N])
        bobs = sb("bobs", [L, D])
        bsum0 = sb("bsum0", [P, 1])
        comp = sb("comp", [P, 2, 2, P])
        wo1 = sb("wo1", [P, B, D])
        ws1 = sb("ws1", [P, B, D])
        const2 = sb("const2", [P, 2])
        bias2 = sb("bias2", [P, 2])
        spa = sb("spa", [P, 4, L])
        nspa = sb("nspa", [P, L])
        gw16 = sb("gw16", [P, 2, E], F16)
        gb = sb("gb", [P, E])
        b3d = sb("b3d", [P, B, D])
        xt = sb("xt", [P, J, B, D])
        stats = sb("stats", [P, 8, 4, 6])
        mv = sb("mv", [P, 8, 4, 2])
        lnv = sb("lnv", [P, 8, 4])
        rstd = sb("rstd", [P, 8, 4])
        nmr = sb("nmr", [P, 8, 4])
        xn = sb("xn", [P, 2, 4, D])
        xnT = sb("xnT", [P, B, S])
        absz = sb("absz", [P, S])
        expz = sb("expz", [P, S])
        logz = sb("logz", [P, S])
        posz = sb("posz", [P, S])
        delta = sb("delta", [P, S])
        decay = sb("decay", [P, S])
        drive = sb("drive", [P, S])
        hs = sb("hs", [P, L, S])
        last = sb("last", [P, P])
        wf = sb("wf", [P, 3, E, D])
        wh = sb("wh", [P, 3, E, D], F16)
        wl = sb("wl", [P, 3, E, D], F16)
        xh = sb("xh", [P, J, 512], F16)
        xl = sb("xl", [P, J, 512], F16)
        r1 = sb("r1", [P, 4, 512])
        h1 = sb("h1", [P, 4, 512], F16)
        l1 = sb("l1", [P, 4, 512], F16)
        r2 = sb("r2", [P, 4, 512])
        h2 = sb("h2", [P, 4, 512], F16)
        l2 = sb("l2", [P, 4, 512], F16)
        T = J * B
        lg = sb("lg", [P, T, E])
        lg2 = sb("lg2", [P, T, E])
        m1 = sb("m1", [P, T])
        m2 = sb("m2", [P, T])
        eq = sb("eq", [P, T, E])
        sc = sb("sc", [P, T, E])
        ms = sb("ms", [P, T])
        top1 = sb("top1", [P, T, E])
        top2 = sb("top2", [P, T, E])
        ex = sb("ex", [P, T, E])
        den = sb("den", [P, T])
        pr = sb("pr", [P, T, 2])
        cw = sb("cw", [P, T, 32])
        cwT = sb("cwT", [P, J, P])

        x_here = [sem(f"x_here{b}") for b in range(B)]
        w_here = [sem(f"w_here{i}") for i in range(3)]
        rows_here, wdi_here, wos_here, bobs_here = sem("rows_here"), sem("wdi_here"), sem("wos_here"), sem("bobs_here")
        blockw_here, gb_here, b3_here = sem("blockw_here"), sem("gb_here"), sem("b3_here")
        pool_const = sem("pool_const")
        ln_stat, ln_log, ln_rstd, ln_nmr, ln_norm, ln_tr, ln_hi, ln_lo = (
            sem(n) for n in ("ln_stat", "ln_log", "ln_rstd", "ln_nmr", "ln_norm", "ln_tr", "ln_hi", "ln_lo"))
        rowsT_mm, cols_done, wosT_mm, wosT_done, comp_mm, comp_done = (
            sem(n) for n in ("rowsT_mm", "cols_done", "wosT_mm", "wosT_done", "comp_mm", "comp_done"))
        a_act, a_done = sem("a_act"), sem("a_done")
        z_mm, z_abs, z_exp, z_log, z_delta, z_decay, z_pos, z_drive, scanned, bias_mm, bias_done = (
            sem(n) for n in ("z_mm", "z_abs", "z_exp", "z_log", "z_delta", "z_decay", "z_pos", "z_drive", "scanned",
                             "bias_mm", "bias_done"))
        last_done, crow_mm, proj_mm, x1_done = sem("last_done"), sem("crow_mm"), sem("proj_mm"), sem("x1_done")
        gate_mm, gate_sub, gate_exp, cw_done, cwT_mm, cwT_done, b3_mm, b3_added = (
            sem(n) for n in ("gate_mm", "gate_sub", "gate_exp", "cw_done", "cwT_mm", "cwT_done", "b3_mm", "b3_added"))
        wh_done, wl_done = sem("wh_done"), sem("wl_done")
        dve = sem("dve")
        z1_mm, z2_mm, y_mm = sem("z1_mm"), sem("z2_mm"), sem("y_mm")
        r1_done, h1_done, l1_done, r2_done, h2_done = (
            sem(n) for n in ("r1_done", "h1_done", "l1_done", "r2_done", "h2_done"))
        l2_pool, l2_dve, y_used = sem("l2_pool"), sem("l2_dve"), sem("y_used")
        stored = sem("stored")

        block = ctx.enter_context(nc.Block())

        def at(item, plus=1):
            c, k = item
            return c * E + (k + plus)

        def back(c, k, lag):
            return (c, k - lag) if k >= lag else (c - 1, k - lag + E)

        def real(item):
            c, k = item
            return not isinstance(c, int) or 0 <= c * E + k < ITEMS

        def wait(eng, s, value):
            if not isinstance(value, int) or value > 0:
                eng.wait_ge(s, value)

        def wait_l2(eng, item, plus=1):
            c, k = item[0], item[1] + plus - 1
            if k < 0:
                c, k = c - 1, k + E
            if isinstance(c, int) and c < 0:
                return
            wait(eng, l2_pool, c * (E // 2) + (k // 2 + 1))
            wait(eng, l2_dve, c * (E // 2) + ((k + 1) // 2))

        def over_items(eng, step, lag):
            for k in range(E):
                step(0, k)
            with eng.Fori(1, J) as c:
                for k in range(E):
                    step(c, k)
            for k in range(lag):
                step(J, k)

        def ln_tile(g, t):
            return xt[:, t, g, :] if g < B else xt[:, g - B, t, :]

        @block.sync
        def _(sp):
            for b in range(B):
                sp.dma_start(xt[:, :, b, :], x_in[b].rearrange("(j p) d -> p j d", p=P)).then_inc(x_here[b], 16)
            for i, w in enumerate((w1, w2, w3)):
                sp.dma_start(wf[:, i, :, :], w.rearrange("e d o -> d e o")).then_inc(w_here[i], 16)
            for c in range(J):
                sp.wait_ge(y_used, (c + 1) * E)
                sp.dma_start(out[:, c * P:(c + 1) * P, :].rearrange("b p d -> p b d"), xt[:, c, :, :]).then_inc(stored, 16)
            sp.wait_ge(stored, 16 * J)

        @block.gpsimd
        def _(pool):
            pool.memset(ident[:, :], 0.0).then_inc(pool_const, 1)
            pool.memset(wo1[:, :, :], 0.0).then_inc(pool_const, 1)
            pool.memset(ws1[:, :, :], 0.0).then_inc(pool_const, 1)
            pool.memset(b3d[:, :, :], 0.0).then_inc(pool_const, 1)
            pool.wait_ge(pool_const, 1)
            pool.affine_select(out=ident[:, :], in_=ident[:, :], compare_op=ALU.not_equal, fill=1.0, base=0,
                               pattern=[[-1, P]], channel_multiplier=1).then_inc(pool_const, 1)
            pool.wait_ge(pool_const, 4)
            for b in range(B):
                pool.dma_start(wo1[b * N:(b + 1) * N, b, :], Wo[1]).then_inc(blockw_here, 16)
                pool.dma_start(ws1[b * N:(b + 1) * N, b, :], Ws[1]).then_inc(blockw_here, 16)
            for b in range(B):
                pool.dma_start(b3d[b * 32:b * 32 + E, b, :], b3).then_inc(b3_here, 16)
            pool.dma_start(gb[:, :], gate_b.partition_broadcast(P)).then_inc(gb_here, 16)
            pool.memset(ones[:, :], 1.0)
            pool.memset(eps[:, :], EPS)
            pool.memset(cw[:, :, :], 0.0)
            for e in range(E):
                done = pool.memset(first[:, e:e + 1], float(E - e))
            done.then_inc(pool_const, 1)
            for i in range(3):
                pool.wait_ge(wh_done, i + 1)
                pool.tensor_tensor(wl[:, i, :, :], wf[:, i, :, :], wh[:, i, :, :], ALU.subtract).then_inc(wl_done, 1)

            def step(c, k):
                item = (c, k)
                if real(item):
                    pool.wait_ge(r1_done, at(item))
                    pool.wait_ge(h1_done, at(item))
                    wait(pool, z2_mm, at(item, -3))
                    pool.tensor_tensor(l1[:, k % 4, :], r1[:, k % 4, :], h1[:, k % 4, :], ALU.subtract).then_inc(l1_done, 1)
                item = back(c, k, 3)
                if real(item) and item[1] % 2 == 0:
                    q = item[1] % 4
                    pool.wait_ge(h2_done, at(item))
                    wait(pool, y_mm, at(item, -3))
                    pool.tensor_tensor(l2[:, q, :], r2[:, q, :], h2[:, q, :], ALU.subtract).then_inc(l2_pool, 1)

            over_items(pool, step, 3)

        @block.scalar
        def _(act):
            act.preload_act_table_set("natural_log_exp_and_others")
            for r, v in ((R_BD, bd), (R_BI, bi), (R_A, A_log)):
                for b in range(B):
                    act.dma_start(rows[r:r + L, b * N:(b + 1) * N], v).then_inc(rows_here, 16)
            for r, v in ((R_B1, b1), (R_B2, b2), (R_GW, gate_w), (R_BO, bo), (R_BS, bs)):
                act.dma_start(rows[r:r + v.shape[0], :], v).then_inc(rows_here, 16)
            act.dma_start(wdi[:, :, 0, :], Wd.rearrange("l d n -> d l n")).then_inc(wdi_here, 16)
            act.dma_start(wdi[:, :, 1, :], Wi.rearrange("l d n -> d l n")).then_inc(wdi_here, 16)
            act.dma_start(wos0[0:N, :], Wo[0]).then_inc(wos_here, 16)
            act.dma_start(wos0[N:2 * N, :], Ws[0]).then_inc(wos_here, 16)
            act.dma_start(bobs[0:1, :], bo[1:2, :]).then_inc(bobs_here, 16)
            act.dma_start(bobs[1:2, :], bs[1:2, :]).then_inc(bobs_here, 16)

            def normalise(g):
                act.wait_ge(ln_stat, g + 1)
                act.activation(lnv[:, g, :], mv[:, g, :, 1], ACT.Ln, bias=eps[:, :]).then_inc(ln_log, 1)
                act.wait_ge(ln_log, g + 1)
                act.activation(rstd[:, g, :], lnv[:, g, :], ACT.Exp, scale=-0.5).then_inc(ln_rstd, 1)
                act.wait_ge(ln_nmr, g + 1)
                if g >= 2:
                    act.wait_ge(ln_tr, g - 1)
                for t in range(4):
                    done = act.activation(xn[:, g % 2, t, :], ln_tile(g, t), ACT.Identity, bias=nmr[:, g, t:t + 1],
                                          scale=rstd[:, g, t:t + 1])
                done.then_inc(ln_norm, 1)

            act.wait_ge(pool_const, 6)
            for g in range(B):
                normalise(g)
                if g >= 1:
                    act.wait_ge(ln_tr, g)
                    act.activation(xnT[:, g - 1, :], TR1[g - 1][:, :], ACT.Copy).then_inc(ln_hi, 1)
            act.wait_ge(ln_tr, B)
            act.activation(xnT[:, B - 1, :], TR1[B - 1][:, :], ACT.Copy).then_inc(ln_hi, 1)

            act.wait_ge(cols_done, 1)
            act.activation(spa[:, 0, :], cols[:, R_A:R_A + L], ACT.Abs).then_inc(a_act, 1)
            act.wait_ge(a_act, 1)
            act.activation(spa[:, 1, :], spa[:, 0, :], ACT.Exp, scale=-1.0).then_inc(a_act, 1)
            act.wait_ge(a_act, 2)
            act.activation(spa[:, 2, :], spa[:, 1, :], ACT.Ln, bias=1.0).then_inc(a_act, 1)

            for l in range(L):
                act.wait_ge(z_mm, l + 1)
                if l == 1:
                    act.wait_ge(bias_done, 1)
                bias_d = cols[:, R_BD:R_BD + 1] if l == 0 else bias2[:, 0:1]
                act.activation(absz[:, :], ZD[:, :], ACT.Abs, bias=bias_d).then_inc(z_abs, 1)
                act.wait_ge(z_abs, l + 1)
                act.activation(expz[:, :], absz[:, :], ACT.Exp, scale=-1.0).then_inc(z_exp, 1)
                act.wait_ge(z_exp, l + 1)
                act.activation(logz[:, :], expz[:, :], ACT.Ln, bias=1.0).then_inc(z_log, 1)
                act.wait_ge(z_delta, l + 1)
                if l == 0:
                    act.wait_ge(a_done, 1)
                act.activation(decay[:, :], delta[:, :], ACT.Exp, scale=nspa[:, l:l + 1]).then_inc(z_decay, 1)
                for i in ((0, 1), (2,))[l]:
                    act.wait_ge(w_here[i], 16)
                    act.activation(wh[:, i, :, :], wf[:, i, :, :], ACT.Copy).then_inc(wh_done, 1)

            def hi(j):
                act.wait_ge(ln_tr, B + j + 1)
                act.activation(xh[:, j, :], TR2[j % 2][:, :], ACT.Copy).then_inc(ln_hi, 1)

            for j in range(J):
                normalise(B + j)
                if j >= 1:
                    hi(j - 1)
            hi(J - 1)
            act.wait_ge(gate_sub, 1)
            act.activation(ex[:, :, :], lg2[:, :, :], ACT.Exp).then_inc(gate_exp, 1)

            def step(c, k):
                item = (c, k)
                if real(item):
                    act.wait_ge(z1_mm, at(item))
                    wait(act, l1_done, at(item, -3))
                    act.activation(r1[:, k % 4, :], Z1[k % 2][:, :], ACT.Relu, bias=cols[:, R_B1 + k:R_B1 + k + 1]).then_inc(r1_done, 1)
                    wait(act, z2_mm, at(item, -3))
                    act.activation(h1[:, k % 4, :], Z1[k % 2][:, :], ACT.Relu, bias=cols[:, R_B1 + k:R_B1 + k + 1]).then_inc(h1_done, 1)
                item = back(c, k, 2)
                if real(item):
                    e = item[1]
                    act.wait_ge(z2_mm, at(item))
                    wait_l2(act, item, -3)
                    act.activation(r2[:, e % 4, :], Z2[e % 2][:, :], ACT.Relu, bias=cols[:, R_B2 + e:R_B2 + e + 1]).then_inc(r2_done, 1)

            over_items(act, step, 2)

        @block.vector
        def _(v):
            steps = [0]

            def then(done):
                steps[0] += 1
                done.then_inc(dve, 1)
                v.wait_ge(dve, steps[0])

            def statistics(g):
                for t in range(4):
                    done = v.bn_stats(stats[:, g, t, :], ln_tile(g, t))
                then(done)
                for t in range(4):
                    done = v.bn_aggr(mv[:, g, t, :], stats[:, g, t, :])
                done.then_inc(ln_stat, 1)

            def shift(g):
                v.wait_ge(ln_rstd, g + 1)
                v.wait_ge(ln_stat, g + 1)
                v.scalar_tensor_tensor(nmr[:, g, :], mv[:, g, :, 0], -1.0, rstd[:, g, :], ALU.mult, ALU.mult).then_inc(ln_nmr, 1)

            then(v.memset(blocks[:, :], 0.0))
            for b in range(B):
                v.memset(blocks[b * N:(b + 1) * N, b * N:(b + 1) * N], 1.0)
            for g in range(B):
                v.wait_ge(x_here[g], 16)
                statistics(g)
                shift(g)

            v.wait_ge(rowsT_mm, 1)
            v.tensor_copy(cols[:, :], MISC[:, 0:ROWS]).then_inc(cols_done, 1)
            v.wait_ge(cols_done, 1)
            v.tensor_tensor(bsum0[:, :], cols[:, R_BO:R_BO + 1], cols[:, R_BS:R_BS + 1], ALU.add)
            then(v.tensor_copy(gw16[:, 0, :], cols[:, R_GW:R_GW + E]))
            v.tensor_tensor(gw16[:, 1, :], cols[:, R_GW:R_GW + E], gw16[:, 0, :], ALU.subtract)
            v.wait_ge(wdi_here, 32)
            v.tensor_copy(wdi1[:, :, :, :], wdi[:, 1, :, :].unsqueeze(2).to_broadcast([P, 2, B, N]))
            v.wait_ge(wosT_mm, 1)
            v.tensor_copy(wosT[:, :, :, :], MISC[:, 64:64 + 2 * N].rearrange("p (w n) -> p w n", w=2).unsqueeze(2).to_broadcast([P, 2, B, N])).then_inc(wosT_done, 1)
            v.wait_ge(a_act, 3)
            then(v.scalar_tensor_tensor(spa[:, 3, :], cols[:, R_A:R_A + L], 0.0, spa[:, 2, :], ALU.max, ALU.add))
            v.tensor_scalar(nspa[:, :], spa[:, 3, :], -1.0, None, ALU.mult).then_inc(a_done, 1)

            for l in range(L):
                v.wait_ge(z_abs, l + 1)
                if l == 1:
                    v.wait_ge(bias_done, 1)
                bias_d = cols[:, R_BD:R_BD + 1] if l == 0 else bias2[:, 0:1]
                bias_i = cols[:, R_BI:R_BI + 1] if l == 0 else bias2[:, 1:2]
                v.tensor_scalar(posz[:, :], ZD[:, :], bias_d, 0.0, ALU.add, ALU.max).then_inc(z_pos, 1)
                v.wait_ge(z_pos, l + 1)
                v.wait_ge(z_log, l + 1)
                v.tensor_tensor(delta[:, :], posz[:, :], logz[:, :], ALU.add).then_inc(z_delta, 1)
                v.wait_ge(z_delta, l + 1)
                v.scalar_tensor_tensor(drive[:, :], ZI[:, :], bias_i, delta[:, :], ALU.add, ALU.mult).then_inc(z_drive, 1)
                v.wait_ge(z_drive, l + 1)
                v.wait_ge(z_decay, l + 1)
                v.tensor_tensor_scan(hs[:, l, :], decay[:, :], drive[:, :], 0.0, ALU.mult, ALU.add).then_inc(scanned, 1)
                if l == 0:
                    v.wait_ge(comp_mm, 1)
                    v.tensor_tensor(comp[:, :, :, :].rearrange("p w k n -> p (w k) n"),
                                    COMP[:, :].rearrange("p (q n) -> p q n", q=4),
                                    blocks[:, :].unsqueeze(1).to_broadcast([P, 4, P]), ALU.mult)
                    v.tensor_tensor(const2[:, :], MISC[:, 128:130], cols[:, R_BD + 1:R_BI + 2:L], ALU.add).then_inc(comp_done, 1)
                    v.wait_ge(comp_done, 1)
                    v.wait_ge(bias_mm, 1)
                    v.tensor_tensor(bias2[:, :], MISC[:, 132:134], const2[:, :], ALU.add).then_inc(bias_done, 1)
            v.wait_ge(scanned, L)
            v.tensor_copy(last[:, :], hs[:, 1, S - 1:S].to_broadcast([P, P])).then_inc(last_done, 1)

            v.wait_ge(crow_mm, 1)
            crow = CROW[:, :].rearrange("p (b d) -> p b d", b=B)
            for j in range(J):
                done = v.tensor_tensor(xt[:, j, :, :], xt[:, j, :, :], crow, ALU.add)
            done.then_inc(x1_done, 1)
            v.wait_ge(x1_done, 1)

            def lo(j):
                v.wait_ge(ln_hi, B + j + 1)
                v.tensor_tensor(xl[:, j, :], TR2[j % 2][:, :], xh[:, j, :], ALU.subtract).then_inc(ln_lo, 1)

            for j in range(J):
                v.wait_ge(proj_mm, j + 1)
                then(v.tensor_tensor(xt[:, j, :, :], xt[:, j, :, :], PROJ[j][:, :].rearrange("p (b d) -> p b d", b=B), ALU.add))
                statistics(B + j)
                shift(B + j)
                if j >= 1:
                    lo(j - 1)
            lo(J - 1)

            def over_e(t):
                return t[:, :].unsqueeze(2).to_broadcast([P, T, E])

            firsts = first[:, :].unsqueeze(1).to_broadcast([P, T, E])
            v.wait_ge(gate_mm, 1)
            v.wait_ge(gb_here, 16)
            then(v.tensor_tensor(lg[:, :, :], GATE[:, 0:T * E].rearrange("p (t e) -> p t e", e=E),
                                 gb[:, :].unsqueeze(1).to_broadcast([P, T, E]), ALU.add))
            then(v.tensor_reduce(m1[:, :], lg[:, :, :], AX.X, ALU.max))
            v.tensor_tensor(lg2[:, :, :], lg[:, :, :], over_e(m1), ALU.subtract).then_inc(gate_sub, 1)
            then(v.tensor_tensor(eq[:, :, :], lg[:, :, :], over_e(m1), ALU.is_equal))
            then(v.tensor_tensor(sc[:, :, :], eq[:, :, :], firsts, ALU.mult))
            then(v.tensor_reduce(ms[:, :], sc[:, :, :], AX.X, ALU.max))
            then(v.tensor_tensor(top1[:, :, :], sc[:, :, :], over_e(ms), ALU.is_equal))
            v.wait_ge(gate_exp, 1)
            then(v.scalar_tensor_tensor(lg2[:, :, :], top1[:, :, :], FAR, lg[:, :, :], ALU.mult, ALU.add))
            then(v.tensor_reduce(m2[:, :], lg2[:, :, :], AX.X, ALU.max))
            then(v.tensor_tensor(eq[:, :, :], lg2[:, :, :], over_e(m2), ALU.is_equal))
            then(v.tensor_tensor(sc[:, :, :], eq[:, :, :], firsts, ALU.mult))
            then(v.tensor_reduce(ms[:, :], sc[:, :, :], AX.X, ALU.max))
            v.tensor_tensor(top2[:, :, :], sc[:, :, :], over_e(ms), ALU.is_equal)
            then(v.tensor_reduce(den[:, :], ex[:, :, :], AX.X, ALU.add))
            then(v.reciprocal(den[:, :], den[:, :]))
            then(v.tensor_tensor(pr[:, :, :], ex[:, :, 0:2], den[:, :].unsqueeze(2).to_broadcast([P, T, 2]), ALU.mult))
            v.tensor_tensor(top1[:, :, :], top1[:, :, :], pr[:, :, 0:1].to_broadcast([P, T, E]), ALU.mult)
            then(v.tensor_tensor(top2[:, :, :], top2[:, :, :], pr[:, :, 1:2].to_broadcast([P, T, E]), ALU.mult))
            v.tensor_tensor(cw[:, :, 0:E], top1[:, :, :], top2[:, :, :], ALU.add).then_inc(cw_done, 1)
            v.wait_ge(cwT_mm, 1)
            v.tensor_copy(cwT[:, :, :], CWT[:, :].rearrange("p (j q) -> p j q", j=J)).then_inc(cwT_done, 1)
            for j in range(J):
                v.wait_ge(b3_mm, j + 1)
                v.tensor_tensor(xt[:, j, :, :], xt[:, j, :, :], B3P[j % 2][:, :].rearrange("p (b d) -> p b d", b=B), ALU.add).then_inc(b3_added, 1)
            v.wait_ge(b3_added, J)
            v.wait_ge(cw_done, 1)

            def step(c, k):
                item = (c, k)
                if real(item):
                    q = k % 4
                    v.wait_ge(r2_done, at(item))
                    wait(v, y_mm, at(item, -3))
                    v.tensor_copy(h2[:, q, :], r2[:, q, :]).then_inc(h2_done, 1)
                    if k % 2 == 1:
                        v.wait_ge(h2_done, at(item))
                        v.tensor_tensor(l2[:, q, :], r2[:, q, :], h2[:, q, :], ALU.subtract).then_inc(l2_dve, 1)
                item = back(c, k, 2)
                if real(item):
                    chunk, e = item
                    v.wait_ge(y_mm, at(item))
                    wait(v, y_used, at(item, 0))
                    for t in range(B):
                        y = xt[:, chunk, t, :]
                        done = v.scalar_tensor_tensor(y, Y[e % 2][:, t * D:(t + 1) * D], cw[:, chunk * B + t, e:e + 1], y, ALU.mult, ALU.add)
                    done.then_inc(y_used, 1)

            over_items(v, step, 2)

        @block.tensor
        def _(pe):
            pe.wait_ge(pool_const, 6)
            pe.wait_ge(rows_here, 16 * 17)
            pe.transpose(MISC[:, 0:ROWS], rows[:, :], ident[0:ROWS, 0:ROWS]).then_inc(rowsT_mm, 1)

            def transposes(g, to):
                pe.wait_ge(ln_norm, g + 1)
                for t in range(4):
                    done = pe.transpose(to[:, t * P:(t + 1) * P], xn[:, g % 2, t, :], ident[:, :])
                done.then_inc(ln_tr, 1)

            for b in range(B):
                transposes(b, TR1[b])
            pe.wait_ge(cols_done, 1)
            pe.wait_ge(wos_here, 32)
            pe.transpose(MISC[:, 64:64 + 2 * N], wos0[:, :], ident[0:2 * N, 0:2 * N]).then_inc(wosT_mm, 1)
            pe.wait_ge(wdi_here, 32)
            for b in range(B):
                pe.wait_ge(ln_hi, b + 1)
                for kind, z in enumerate((ZD, ZI)):
                    done = pe.matmul(z[b * N:(b + 1) * N, :], wdi[:, 0, kind, :], xnT[:, b, :], start=True, stop=True)
            done.then_inc(z_mm, 1)
            pe.wait_ge(wosT_done, 1)
            for w in range(2):
                pe.matmul(COMP[:, w * 2 * P:(w + 1) * 2 * P], wosT[:, w, :, :], wdi1[:, :, :, :], start=True, stop=True)
            for kind in range(2):
                done = pe.matmul(MISC[:, 128 + kind:129 + kind], wdi1[:, kind, :, :], bsum0[:, :], start=True, stop=True)
            done.then_inc(comp_mm, 1)
            pe.wait_ge(comp_done, 1)
            pe.wait_ge(scanned, 1)
            pe.wait_ge(z_drive, 1)
            for kind in range(2):
                done = pe.matmul(MISC[:, 132 + kind:133 + kind], comp[:, 1, kind, :], hs[:, 0, S - 1:S], start=True, stop=True)
            done.then_inc(bias_mm, 1)
            for kind, z in enumerate((ZD, ZI)):
                done = pe.matmul(z[:, :], comp[:, 0, kind, :], hs[:, 0, :], start=True, stop=True)
            done.then_inc(z_mm, 1)
            pe.wait_ge(bobs_here, 32)
            pe.wait_ge(blockw_here, 16 * 2 * B)
            pe.wait_ge(bias_done, 1)
            for b in range(B):
                pe.matmul(CROW[:, b * D:(b + 1) * D], ones[:, :], bobs[:, :], start=b == 0, stop=False, skip_group_check=True)
            pe.wait_ge(last_done, 1)
            pe.matmul(CROW[:, :], last[:, :], ws1[:, :, :], start=False, stop=True, skip_group_check=True).then_inc(crow_mm, 1)
            for j in range(J):
                pe.matmul(PROJ[j][:, :], hs[:, 1, j * P:(j + 1) * P], wo1[:, :, :], start=True, stop=True).then_inc(proj_mm, 1)

            def gate(j):
                pe.wait_ge(ln_lo, j + 1)
                for t in range(4):
                    to = GATE[:, (j * B + t) * E:(j * B + t + 1) * E]
                    tok = slice(t * P, (t + 1) * P)
                    pe.matmul(to, xh[:, j, tok], gw16[:, 0, :], start=True, stop=False)
                    pe.matmul(to, xl[:, j, tok], gw16[:, 0, :], start=False, stop=False)
                    done = pe.matmul(to, xh[:, j, tok], gw16[:, 1, :], start=False, stop=True)
                return done

            pe.wait_ge(x1_done, 1)
            for j in range(J):
                if j >= 2:
                    pe.wait_ge(ln_lo, j - 1)
                transposes(B + j, TR2[j % 2])
            pe.wait_ge(ln_stat, B + J)
            for j in range(J):
                done = gate(j)
            done.then_inc(gate_mm, 1)

            def step(c, k):
                item = (c, k)
                if real(item):
                    wait(pe, r1_done, at(item, -1))
                    wait(pe, h1_done, at(item, -1))
                    z = Z1[k % 2][:, :]
                    pe.matmul(z, wh[:, 0, k, :], xh[:, c, :], start=True, stop=False)
                    pe.matmul(z, wl[:, 0, k, :], xh[:, c, :], start=False, stop=False)
                    pe.matmul(z, wh[:, 0, k, :], xl[:, c, :], start=False, stop=True).then_inc(z1_mm, 1)
                item = back(c, k, 2)
                if real(item):
                    e, q = item[1], item[1] % 4
                    wait(pe, r2_done, at(item, -1))
                    pe.wait_ge(h1_done, at(item))
                    z = Z2[e % 2][:, :]
                    pe.matmul(z, wh[:, 1, e, :], h1[:, q, :], start=True, stop=False)
                    pe.matmul(z, wl[:, 1, e, :], h1[:, q, :], start=False, stop=False)
                    pe.wait_ge(l1_done, at(item))
                    pe.matmul(z, wh[:, 1, e, :], l1[:, q, :], start=False, stop=True).then_inc(z2_mm, 1)
                item = back(c, k, 4)
                if real(item):
                    e, q = item[1], item[1] % 4
                    wait(pe, y_used, at(item, -1))
                    pe.wait_ge(h2_done, at(item))
                    wait_l2(pe, item)
                    for t in range(4):
                        y, tok = Y[e % 2][:, t * D:(t + 1) * D], slice(t * P, (t + 1) * P)
                        pe.matmul(y, h2[:, q, tok], wh[:, 2, e, :], start=True, stop=False)
                        pe.matmul(y, h2[:, q, tok], wl[:, 2, e, :], start=False, stop=False)
                        done = pe.matmul(y, l2[:, q, tok], wh[:, 2, e, :], start=False, stop=True)
                    done.then_inc(y_mm, 1)

            pe.wait_ge(wl_done, 3)
            pe.wait_ge(b3_here, 16 * B)

            def first_steps(c, k):
                step(c, k)
                if isinstance(c, int) and c == 0 and k == 1:
                    pe.wait_ge(cw_done, 1)
                    for j in range(J):
                        done = pe.transpose(CWT[:, j * P:(j + 1) * P], cw[:, j * B:(j + 1) * B, :], ident[:, :])
                    done.then_inc(cwT_mm, 1)
                    pe.wait_ge(cwT_done, 1)
                    for j in range(J):
                        if j >= 2:
                            pe.wait_ge(b3_added, j - 1)
                        pe.matmul(B3P[j % 2][:, :], cwT[:, j, :], b3d[:, :, :], start=True, stop=True).then_inc(b3_mm, 1)

            over_items(pe, first_steps, 4)


_INS = ["L0_attn_shot_embeddings", "L0_attn_Wd", "L0_attn_bd", "L0_attn_Wi", "L0_attn_bi", "L0_attn_A_log", "L0_attn_Wo",
        "L0_attn_bo", "L0_attn_Ws", "L0_attn_bs", "L0_ffn_gate_w", "L0_ffn_gate_b", "L0_ffn_w1", "L0_ffn_b1", "L0_ffn_w2",
        "L0_ffn_b2", "L0_ffn_w3", "L0_ffn_b3"]


def kernel(**inputs):
    import numpy as _np
    import concourse.bacc as _bacc
    from concourse.bass_utils import run_bass_kernel_spmd as _run

    nc = _bacc.Bacc("TRN2", target_bir_lowering=False, num_devices=1)
    arrays, args = {}, []
    for name in _INS:
        a = _np.ascontiguousarray(inputs[name])
        arrays[f"in_{name}"] = a
        args.append(nc.dram_tensor(f"in_{name}", a.shape, mybir.dt.from_np(a.dtype), kind="ExternalInput").ap())
    args.append(nc.dram_tensor("result", [B, S, D], F32, kind="ExternalOutput").ap())
    program(nc, *args)
    r = _run(nc, [arrays], core_ids=[0])
    return r.results[0]["result"]
```

```python
from contextlib import ExitStack

import concourse.bass as bass
from concourse import mybir

F32 = mybir.dt.float32
F16 = mybir.dt.float16
ALU = mybir.AluOpType
ACT = mybir.ActivationFunctionType
AX = mybir.AxisListType

P = 128
B, S, D = 4, 512, 128
N = 32
L = 2
E = 8
J = S // P
ITEMS = J * E
EPS = 1e-5
GSTEPS = 18
FAR = -1e30

R_B1, R_B2, R_GW, R_BO, R_BS, R_BD, R_BI, R_A = 0, E, 2 * E, 3 * E, 3 * E + L, 3 * E + 2 * L, 3 * E + 3 * L, 3 * E + 4 * L
ROWS = 3 * E + 5 * L


def program(nc, x_in, Wd, bd, Wi, bi, A_log, Wo, bo, Ws, bs, gate_w, gate_b, w1, b1, w2, b2, w3, b3, out):
    with ExitStack() as ctx:
        def sb(name, shape, dt=F32):
            return ctx.enter_context(nc.sbuf_tensor(name, shape, dt))

        def sem(name):
            return ctx.enter_context(nc.semaphore(name))

        bank = [ctx.enter_context(nc.psum_tensor(f"bank{i}", [P, 512], F32)) for i in range(8)]
        ZD, ZI = bank[0], bank[1]
        XT = bank[2:6]
        RB = bank[2]
        PROJ = bank[2:6]
        MISC = bank[6]
        WCEN, COMP = bank[7], bank[7]
        CROW = bank[6]
        TR2 = [bank[7], bank[6], bank[6], bank[6]]
        GATE, CWT, B3P = bank[7], bank[7], [bank[6], bank[6], bank[6], bank[7]]
        Z1, Z2, Y = bank[0:2], bank[2:4], bank[4:6]

        ident = sb("ident", [P, P])
        centre = sb("centre", [P, P])
        of_batch = sb("of_batch", [P, B])
        of_tile = sb("of_tile", [B * E, B])
        ones = sb("ones", [L, P])
        eps = sb("eps", [P, 1])
        first = sb("first", [P, E])
        rows = sb("rows", [ROWS, P])
        cols = sb("cols", [P, ROWS])
        wdi = sb("wdi", [P, L, 2, N])
        wcen = sb("wcen", [P, 2, N])
        wos0 = sb("wos0", [2 * N, D])
        wosT = sb("wosT", [P, 2, B, N])
        wdi1 = sb("wdi1", [P, 2, B, N])
        bobs = sb("bobs", [L, D])
        bsum0 = sb("bsum0", [P, 1])
        comp = sb("comp", [P, 2, 2, P])
        wos1 = sb("wos1", [P, 2, D])
        wo1 = sb("wo1", [P, B, D])
        ws1 = sb("ws1", [P, B, D])
        const2 = sb("const2", [P, 2])
        bias2 = sb("bias2", [P, 2])
        spa = sb("spa", [P, 4, L])
        nspa = sb("nspa", [P, L])
        gw16 = sb("gw16", [P, 2, E], F16)
        gb = sb("gb", [P, E])
        b3r = sb("b3r", [B * E, D])
        b3d = sb("b3d", [B * E, B, D])
        xt = sb("xt", [P, J, B, D])
        stats = sb("stats", [P, B, J, 6])
        var = sb("var", [P, 4, B, J])
        lnv1 = sb("lnv1", [P, B, J])
        rstd1 = sb("rstd1", [P, B, J])
        rexp = sb("rexp", [P, J, B, N])
        rb = sb("rb", [P, S])
        xT = sb("xT", [P, B, S])
        stats2 = sb("stats2", [P, J, B, 6])
        mv = sb("mv", [P, J, B, 2])
        lnv = sb("lnv", [P, J, B])
        rstd = sb("rstd", [P, J, B])
        nmr = sb("nmr", [P, J, B])
        xn = sb("xn", [P, 2, B, D])
        crow = sb("crow", [P, B, D])
        zd = sb("zd", [P, S])
        zi = sb("zi", [P, S])
        absz = sb("absz", [P, S])
        expz = sb("expz", [P, S])
        logz = sb("logz", [P, S])
        posz = sb("posz", [P, S])
        delta = sb("delta", [P, S])
        decay = sb("decay", [P, S])
        drive = sb("drive", [P, S])
        hs = sb("hs", [P, L, S])
        last = sb("last", [P, P])
        wf = sb("wf", [P, 3, E, D])
        wh = sb("wh", [P, 3, E, D], F16)
        wl = sb("wl", [P, 3, E, D], F16)
        xh = sb("xh", [P, J, 512], F16)
        xl = sb("xl", [P, J, 512], F16)
        r1 = sb("r1", [P, 4, 512])
        h1 = sb("h1", [P, 4, 512], F16)
        l1 = sb("l1", [P, 4, 512], F16)
        r2 = sb("r2", [P, 4, 512])
        h2 = sb("h2", [P, 4, 512], F16)
        l2 = sb("l2", [P, 4, 512], F16)
        T = J * B
        lg = sb("lg", [P, T, E])
        dl = sb("dl", [P, T, E])
        m1 = sb("m1", [P, T])
        m2 = sb("m2", [P, T])
        eq = sb("eq", [P, T, E])
        sc = sb("sc", [P, T, E])
        ms = sb("ms", [P, T])
        top1 = sb("top1", [P, T, E])
        top2 = sb("top2", [P, T, E])
        ex = sb("ex", [P, T, E])
        den = sb("den", [P, T])
        pr = sb("pr", [P, T, 2])
        cw = sb("cw", [P, T, E])
        cwT = sb("cwT", [B * E, J, P])

        x_here = [sem(f"x_here{b}") for b in range(B)]
        w_here = [sem(f"w_here{i}") for i in range(3)]
        rows_here, wdi_here, wos_here, bobs_here, wos1_here, gb_here, b3_here = (
            sem(n) for n in ("rows_here", "wdi_here", "wos_here", "bobs_here", "wos1_here", "gb_here", "b3_here"))
        ident_done, pool_const, centre_done, masks_done, blocks_done = (
            sem(n) for n in ("ident_done", "pool_const", "centre_done", "masks_done", "blocks_done"))
        rowsT_mm, cols_done, wcen_mm, wcen_done, wosT_mm, wosT_done, comp_mm, comp_done = (
            sem(n) for n in ("rowsT_mm", "cols_done", "wcen_mm", "wcen_done", "wosT_mm", "wosT_done", "comp_mm", "comp_done"))
        xT_mm, xT_done, var_done, lnv1_done, rstd1_done, rexp_done, rb_mm, rb_done = (
            sem(n) for n in ("xT_mm", "xT_done", "var_done", "lnv1_done", "rstd1_done", "rexp_done", "rb_mm", "rb_done"))
        a_act, a_done = sem("a_act"), sem("a_done")
        zd_mm, zi_mm, zd_done, zi_done, z_abs, z_exp, z_log, z_pos, z_delta, z_decay, z_drive, scanned = (
            sem(n) for n in ("zd_mm", "zi_mm", "zd_done", "zi_done", "z_abs", "z_exp", "z_log", "z_pos", "z_delta", "z_decay",
                             "z_drive", "scanned"))
        bias_mm, bias_done = sem("bias_mm"), sem("bias_done")
        last_done, crow_mm, crow_read, crow_done, crow_added, proj_mm = (
            sem(n) for n in ("last_done", "crow_mm", "crow_read", "crow_done", "crow_added", "proj_mm"))
        ln_stat, ln_log, ln_rstd, ln_nmr, norm_act, norm_pool, ln_tr, ln_hi, ln_lo = (
            sem(n) for n in ("ln_stat", "ln_log", "ln_rstd", "ln_nmr", "norm_act", "norm_pool", "ln_tr", "ln_hi", "ln_lo"))
        gate_mm, gate_step, gate_exp, cwT_mm, cwT_done, b3_mm, b3_added = (
            sem(n) for n in ("gate_mm", "gate_step", "gate_exp", "cwT_mm", "cwT_done", "b3_mm", "b3_added"))
        wh_done, wl_done = sem("wh_done"), sem("wl_done")
        dve = sem("dve")
        z1_mm, z2_mm, y_mm = sem("z1_mm"), sem("z2_mm"), sem("y_mm")
        r1_done, h1_done, l1_done, r2_done, h2_done = (
            sem(n) for n in ("r1_done", "h1_done", "l1_done", "r2_done", "h2_done"))
        l2_pool, l2_dve, y_used = sem("l2_pool"), sem("l2_dve"), sem("y_used")
        stored = sem("stored")

        block = ctx.enter_context(nc.Block())

        def at(item, plus=1):
            c, k = item
            return c * E + (k + plus)

        def back(c, k, lag):
            return (c, k - lag) if k >= lag else (c - 1, k - lag + E)

        def real(item):
            c, k = item
            return not isinstance(c, int) or 0 <= c * E + k < ITEMS

        def wait(eng, s, value):
            if not isinstance(value, int) or value > 0:
                eng.wait_ge(s, value)

        def wait_l2(eng, item, plus=1):
            c, k = item[0], item[1] + plus - 1
            if k < 0:
                c, k = c - 1, k + E
            if isinstance(c, int) and c < 0:
                return
            wait(eng, l2_pool, c * (E // 2) + (k // 2 + 1))
            wait(eng, l2_dve, c * (E // 2) + ((k + 1) // 2))

        def over_items(eng, step, lag):
            for k in range(E):
                step(0, k)
            with eng.Fori(1, J) as c:
                for k in range(E):
                    step(c, k)
            for k in range(lag):
                step(J, k)

        HALVES = [slice(0, S // 2), slice(S // 2, S)]

        def by_batch(psum):
            return psum[:, :].rearrange("p (b d) -> p b d", b=B)

        @block.sync
        def _(sp):
            for b in range(B):
                sp.dma_start(xt[:, :, b, :], x_in[b].rearrange("(j p) d -> p j d", p=P)).then_inc(x_here[b], 16)
            sp.dma_start(wos0[0:N, :], Wo[0]).then_inc(wos_here, 16)
            sp.dma_start(wos0[N:2 * N, :], Ws[0]).then_inc(wos_here, 16)
            for i, w in enumerate((w1, w2, w3)):
                sp.dma_start(wf[:, i, :, :], w.rearrange("e d o -> d e o")).then_inc(w_here[i], 16)
            for c in range(J):
                sp.wait_ge(y_used, (c + 1) * E)
                sp.dma_start(out[:, c * P:(c + 1) * P, :].rearrange("b p d -> p b d"), xt[:, c, :, :]).then_inc(stored, 16)
            sp.wait_ge(stored, 16 * J)

        @block.gpsimd
        def _(pool):
            pool.memset(ident[:, :], 0.0).then_inc(ident_done, 1)
            pool.wait_ge(ident_done, 1)
            pool.affine_select(out=ident[:, :], in_=ident[:, :], compare_op=ALU.not_equal, fill=1.0, base=0,
                               pattern=[[-1, P]], channel_multiplier=1).then_inc(ident_done, 1)
            for w, v in enumerate((Wo, Ws)):
                pool.dma_start(wos1[:, w, :], v[1].partition_broadcast(B)).then_inc(wos1_here, 16)
            pool.dma_start(b3r[:, :], b3.partition_broadcast(B)).then_inc(b3_here, 16)
            pool.dma_start(gb[:, :], gate_b.partition_broadcast(P)).then_inc(gb_here, 16)
            pool.dma_start(bobs[0:1, :], bo[1:2, :]).then_inc(bobs_here, 16)
            pool.dma_start(bobs[1:2, :], bs[1:2, :]).then_inc(bobs_here, 16)
            pool.wait_ge(masks_done, 2)
            pool.wait_ge(wos1_here, 32)
            for w, to in enumerate((wo1, ws1)):
                pool.tensor_tensor(to[:, :, :], wos1[:, w, :].unsqueeze(1).to_broadcast([P, B, D]),
                                   of_batch[:, :].unsqueeze(2).to_broadcast([P, B, D]), ALU.mult).then_inc(blocks_done, 1)
            pool.wait_ge(b3_here, 16)
            pool.wait_ge(blocks_done, 2)
            pool.tensor_tensor(b3d[:, :, :], b3r[:, :].unsqueeze(1).to_broadcast([B * E, B, D]),
                               of_tile[:, :].unsqueeze(2).to_broadcast([B * E, B, D]), ALU.mult).then_inc(blocks_done, 1)
            for i in range(3):
                pool.wait_ge(wh_done, i + 1)
                pool.tensor_tensor(wl[:, i, :, :], wf[:, i, :, :], wh[:, i, :, :], ALU.subtract).then_inc(wl_done, 1)
            pool.wait_ge(crow_done, 1)

            def add_crow(j):
                pool.tensor_tensor(xt[:, j, :, :], xt[:, j, :, :], crow[:, :, :], ALU.add).then_inc(crow_added, 1)

            def normalise(j):
                pool.wait_ge(ln_nmr, j + 1)
                if j >= 2:
                    pool.wait_ge(ln_tr, j - 1)
                for t in (2, 3):
                    done = pool.tensor_scalar(xn[:, j % 2, t, :], xt[:, j, t, :], rstd[:, j, t:t + 1], nmr[:, j, t:t + 1],
                                              ALU.mult, ALU.add)
                done.then_inc(norm_pool, 1)

            add_crow(1)
            normalise(0)
            add_crow(2)
            add_crow(3)
            normalise(1)

            def step(c, k):
                item = (c, k)
                first_chunk = isinstance(c, int) and c == 0
                if first_chunk and k in (1, 2):
                    normalise(k + 1)
                if real(item):
                    pool.wait_ge(r1_done, at(item))
                    pool.wait_ge(h1_done, at(item))
                    wait(pool, z2_mm, at(item, -3))
                    pool.tensor_tensor(l1[:, k % 4, :], r1[:, k % 4, :], h1[:, k % 4, :], ALU.subtract).then_inc(l1_done, 1)
                item = back(c, k, 2)
                if real(item) and item[1] % 2 == 0:
                    q = item[1] % 4
                    pool.wait_ge(h2_done, at(item))
                    wait(pool, y_mm, at(item, -3))
                    pool.tensor_tensor(l2[:, q, :], r2[:, q, :], h2[:, q, :], ALU.subtract).then_inc(l2_pool, 1)

            over_items(pool, step, 2)

        @block.scalar
        def _(act):
            act.dma_start(wdi[:, :, 0, :], Wd.rearrange("l d n -> d l n")).then_inc(wdi_here, 16)
            act.dma_start(wdi[:, :, 1, :], Wi.rearrange("l d n -> d l n")).then_inc(wdi_here, 16)
            for r, v in ((R_BD, bd), (R_BI, bi), (R_A, A_log)):
                act.dma_start(rows[r:r + L, :].rearrange("l (b n) -> l b n", b=B),
                              v.unsqueeze(1).to_broadcast([L, B, N])).then_inc(rows_here, 16)
            for r, v in ((R_B1, b1), (R_B2, b2), (R_GW, gate_w), (R_BO, bo), (R_BS, bs)):
                act.dma_start(rows[r:r + v.shape[0], :], v).then_inc(rows_here, 16)
            act.preload_act_table_set("natural_log_exp_and_others")

            for b in range(B):
                act.wait_ge(xT_mm, b + 1)
                act.activation(xT[:, b, :], XT[b][:, :], ACT.Copy).then_inc(xT_done, 1)
            act.wait_ge(var_done, 4)
            act.activation(lnv1[:, :, :], var[:, 3, :, :], ACT.Ln, bias=eps[:, :], scale=1.0 / D).then_inc(lnv1_done, 1)
            act.wait_ge(lnv1_done, 1)
            act.activation(rstd1[:, :, :], lnv1[:, :, :], ACT.Exp, scale=-0.5).then_inc(rstd1_done, 1)

            act.wait_ge(cols_done, 1)
            act.activation(spa[:, 0, :], cols[:, R_A:R_A + L], ACT.Abs).then_inc(a_act, 1)
            act.wait_ge(a_act, 1)
            act.activation(spa[:, 1, :], spa[:, 0, :], ACT.Exp, scale=-1.0).then_inc(a_act, 1)
            act.wait_ge(a_act, 2)
            act.activation(spa[:, 2, :], spa[:, 1, :], ACT.Ln, bias=1.0).then_inc(a_act, 1)
            act.wait_ge(rb_mm, 1)
            act.activation(rb[:, :], RB[:, :], ACT.Copy).then_inc(rb_done, 1)

            for l in range(L):
                z, bias_d = (zd, cols[:, R_BD:R_BD + 1]) if l == 0 else (ZD, bias2[:, 0:1])
                if l == 0:
                    act.wait_ge(zd_done, 1)
                else:
                    act.wait_ge(zd_mm, 3)
                    act.wait_ge(bias_done, 1)
                for i, h in enumerate(HALVES):
                    act.activation(absz[:, h], z[:, h], ACT.Abs, bias=bias_d).then_inc(z_abs, 1)
                for i, h in enumerate(HALVES):
                    act.wait_ge(z_abs, 2 * l + i + 1)
                    act.activation(expz[:, h], absz[:, h], ACT.Exp, scale=-1.0).then_inc(z_exp, 1)
                for i, h in enumerate(HALVES):
                    act.wait_ge(z_exp, 2 * l + i + 1)
                    act.activation(logz[:, h], expz[:, h], ACT.Ln, bias=1.0).then_inc(z_log, 1)
                if l == 0:
                    act.wait_ge(a_done, 1)
                for i, h in enumerate(HALVES):
                    act.wait_ge(z_delta, 2 * l + i + 1)
                    act.activation(decay[:, h], delta[:, h], ACT.Exp, scale=nspa[:, l:l + 1]).then_inc(z_decay, 1)
                for i in ((0, 1), (2,))[l]:
                    act.wait_ge(w_here[i], 16)
                    act.activation(wh[:, i, :, :], wf[:, i, :, :], ACT.Copy).then_inc(wh_done, 1)

            act.wait_ge(crow_read, 1)
            act.activation(crow[:, :, :], by_batch(CROW), ACT.Copy).then_inc(crow_done, 1)

            def rstd_of(j):
                act.wait_ge(ln_stat, j + 1)
                act.activation(lnv[:, j, :], mv[:, j, :, 1], ACT.Ln, bias=eps[:, :]).then_inc(ln_log, 1)
                act.wait_ge(ln_log, j + 1)
                act.activation(rstd[:, j, :], lnv[:, j, :], ACT.Exp, scale=-0.5).then_inc(ln_rstd, 1)

            def normalise(j):
                act.wait_ge(ln_nmr, j + 1)
                if j >= 2:
                    act.wait_ge(ln_tr, j - 1)
                for t in (0, 1):
                    done = act.activation(xn[:, j % 2, t, :], xt[:, j, t, :], ACT.Identity, bias=nmr[:, j, t:t + 1],
                                          scale=rstd[:, j, t:t + 1])
                done.then_inc(norm_act, 1)

            def high(j):
                act.wait_ge(ln_tr, j + 1)
                act.activation(xh[:, j, :], TR2[j][:, :], ACT.Copy).then_inc(ln_hi, 1)

            def gate_exps(h):
                tiles = slice(h * T // 2, (h + 1) * T // 2)
                act.wait_ge(gate_step, GSTEPS * h + 3)
                act.activation(ex[:, tiles, :], dl[:, tiles, :], ACT.Exp).then_inc(gate_exp, 1)

            rstd_of(0)
            normalise(0)
            rstd_of(1)
            high(0)
            normalise(1)
            high(1)

            def step(c, k):
                item = (c, k)
                first_chunk = isinstance(c, int) and c == 0
                if real(item):
                    act.wait_ge(z1_mm, at(item))
                    wait(act, l1_done, at(item, -3))
                    bias = cols[:, R_B1 + k:R_B1 + k + 1]
                    act.activation(r1[:, k % 4, :], Z1[k % 2][:, :], ACT.Relu, bias=bias).then_inc(r1_done, 1)
                    wait(act, z2_mm, at(item, -3))
                    act.activation(h1[:, k % 4, :], Z1[k % 2][:, :], ACT.Relu, bias=bias).then_inc(h1_done, 1)
                if first_chunk and k == 0:
                    rstd_of(2)
                    gate_exps(0)
                if first_chunk and k == 1:
                    normalise(2)
                    rstd_of(3)
                item = back(c, k, 2)
                if real(item):
                    e = item[1]
                    act.wait_ge(z2_mm, at(item))
                    wait_l2(act, item, -3)
                    act.activation(r2[:, e % 4, :], Z2[e % 2][:, :], ACT.Relu, bias=cols[:, R_B2 + e:R_B2 + e + 1]).then_inc(r2_done, 1)
                if first_chunk and k == 2:
                    normalise(3)
                    high(2)
                if first_chunk and k == 3:
                    high(3)
                if first_chunk and k == 5:
                    gate_exps(1)

            over_items(act, step, 2)

        @block.vector
        def _(v):
            steps = [0]

            def then(done):
                steps[0] += 1
                done.then_inc(dve, 1)
                v.wait_ge(dve, steps[0])

            v.memset(ones[:, :], 1.0)
            v.memset(eps[:, :], EPS)
            for e in range(E):
                done = v.memset(first[:, e:e + 1], float(E - e))
            done.then_inc(pool_const, 1)
            v.wait_ge(ident_done, 2)
            v.tensor_scalar(centre[:, :], ident[:, :], -1.0 / D, None, ALU.add).then_inc(centre_done, 1)
            v.tensor_reduce(of_batch[:, :], ident[:, :].rearrange("p (b n) -> p b n", b=B), AX.X, ALU.add).then_inc(masks_done, 1)
            v.tensor_reduce(of_tile[:, :], ident[0:B * E, 0:B * E].rearrange("p (t e) -> p t e", t=B), AX.X, ALU.add).then_inc(masks_done, 1)

            for b in range(B):
                v.wait_ge(x_here[b], 16)
                for j in range(J):
                    done = v.bn_stats(stats[:, b, j, :], xt[:, j, b, :])
                if b == 1:
                    v.wait_ge(wcen_mm, 1)
                    v.tensor_copy(wcen[:, :, :], WCEN[:, 0:2 * N].rearrange("p (w n) -> p w n", w=2)).then_inc(wcen_done, 1)
            then(done)
            v.tensor_tensor(var[:, 0, :, :], stats[:, :, :, 2], stats[:, :, :, 5], ALU.add).then_inc(var_done, 1)
            v.tensor_tensor(var[:, 1, :, :], stats[:, :, :, 1], stats[:, :, :, 4], ALU.subtract).then_inc(var_done, 1)
            v.wait_ge(var_done, 2)
            v.tensor_tensor(var[:, 2, :, :], var[:, 1, :, :], var[:, 1, :, :], ALU.mult).then_inc(var_done, 1)
            v.wait_ge(var_done, 3)
            v.scalar_tensor_tensor(var[:, 3, :, :], var[:, 2, :, :], D / 4.0, var[:, 0, :, :], ALU.mult, ALU.add).then_inc(var_done, 1)
            v.wait_ge(rowsT_mm, 1)
            v.tensor_copy(cols[:, :], MISC[:, 0:ROWS]).then_inc(cols_done, 1)
            v.wait_ge(rstd1_done, 1)
            v.tensor_copy(rexp[:, :, :, :], rstd1[:, :, :].rearrange("p b j -> p j b").unsqueeze(3).to_broadcast([P, J, B, N])).then_inc(rexp_done, 1)
            v.wait_ge(cols_done, 1)
            v.tensor_tensor(bsum0[:, :], cols[:, R_BO:R_BO + 1], cols[:, R_BS:R_BS + 1], ALU.add)
            v.tensor_copy(wdi1[:, :, :, :], wdi[:, 1, :, :].unsqueeze(2).to_broadcast([P, 2, B, N]))
            v.wait_ge(wosT_mm, 1)
            v.tensor_copy(wosT[:, :, :, :], MISC[:, 64:64 + 2 * N].rearrange("p (w n) -> p w n", w=2).unsqueeze(2).to_broadcast([P, 2, B, N])).then_inc(wosT_done, 1)

            for l in range(L):
                if l == 0:
                    v.wait_ge(rb_done, 1)
                    v.wait_ge(zd_mm, 1)
                    v.tensor_tensor(zd[:, :], ZD[:, :], rb[:, :], ALU.mult).then_inc(zd_done, 1)
                    v.wait_ge(zi_mm, 1)
                    v.tensor_tensor(zi[:, :], ZI[:, :], rb[:, :], ALU.mult).then_inc(zi_done, 1)
                    then(v.tensor_copy(gw16[:, 0, :], cols[:, R_GW:R_GW + E]))
                    v.tensor_tensor(gw16[:, 1, :], cols[:, R_GW:R_GW + E], gw16[:, 0, :], ALU.subtract)
                    v.wait_ge(a_act, 3)
                    then(v.scalar_tensor_tensor(spa[:, 3, :], cols[:, R_A:R_A + L], 0.0, spa[:, 2, :], ALU.max, ALU.add))
                    v.tensor_scalar(nspa[:, :], spa[:, 3, :], -1.0, None, ALU.mult).then_inc(a_done, 1)
                    zd_, zi_, bias_d, bias_i = zd, zi, cols[:, R_BD:R_BD + 1], cols[:, R_BI:R_BI + 1]
                    v.wait_ge(zd_done, 1)
                else:
                    zd_, zi_, bias_d, bias_i = ZD, ZI, bias2[:, 0:1], bias2[:, 1:2]
                    v.wait_ge(z_abs, 4)
                v.tensor_scalar(posz[:, :], zd_[:, :], bias_d, 0.0, ALU.add, ALU.max).then_inc(z_pos, 1)
                if l == 0:
                    v.wait_ge(zi_done, 1)
                else:
                    v.wait_ge(zi_mm, 3)
                v.wait_ge(z_pos, l + 1)
                for i, h in enumerate(HALVES):
                    n = 2 * l + i + 1
                    v.wait_ge(z_log, n)
                    v.tensor_tensor(delta[:, h], posz[:, h], logz[:, h], ALU.add).then_inc(z_delta, 1)
                    v.wait_ge(z_delta, n)
                    v.scalar_tensor_tensor(drive[:, h], zi_[:, h], bias_i, delta[:, h], ALU.add, ALU.mult).then_inc(z_drive, 1)
                for i, h in enumerate(HALVES):
                    n = 2 * l + i + 1
                    v.wait_ge(z_drive, n)
                    v.wait_ge(z_decay, n)
                    if i == 1:
                        v.wait_ge(scanned, n - 1)
                    v.tensor_tensor_scan(hs[:, l, h], decay[:, h], drive[:, h],
                                         0.0 if i == 0 else hs[:, l, h.start - 1:h.start], ALU.mult, ALU.add).then_inc(scanned, 1)
                    if l == 0 and i == 0:
                        v.wait_ge(comp_mm, 1)
                        for w in range(2):
                            v.tensor_tensor(comp[:, w, :, :].rearrange("p k (b n) -> p k b n", b=B),
                                            COMP[:, w * 2 * P:(w + 1) * 2 * P].rearrange("p (k b n) -> p k b n", k=2, b=B),
                                            of_batch[:, :].unsqueeze(1).unsqueeze(3).to_broadcast([P, 2, B, N]), ALU.mult)
                        v.tensor_tensor(const2[:, :], MISC[:, 128:130], cols[:, R_BD + 1:R_BI + 2:L], ALU.add).then_inc(comp_done, 1)
                if l == 0:
                    v.wait_ge(comp_done, 1)
                    v.wait_ge(bias_mm, 1)
                    v.tensor_tensor(bias2[:, :], MISC[:, 132:134], const2[:, :], ALU.add).then_inc(bias_done, 1)
            v.wait_ge(scanned, 2 * L)
            v.tensor_copy(last[:, :], hs[:, 1, S - 1:S].to_broadcast([P, P])).then_inc(last_done, 1)

            def add_proj(j):
                if j >= 1:
                    v.wait_ge(crow_added, j)
                v.wait_ge(proj_mm, j + 1)
                then(v.tensor_tensor(xt[:, j, :, :], xt[:, j, :, :], by_batch(PROJ[j]), ALU.add))

            def statistics(j):
                for t in range(B):
                    done = v.bn_stats(stats2[:, j, t, :], xt[:, j, t, :])
                then(done)
                for t in range(B):
                    done = v.bn_aggr(mv[:, j, t, :], stats2[:, j, t, :])
                done.then_inc(ln_stat, 1)

            def shift(j):
                v.wait_ge(ln_rstd, j + 1)
                v.wait_ge(ln_stat, j + 1)
                v.scalar_tensor_tensor(nmr[:, j, :], mv[:, j, :, 0], -1.0, rstd[:, j, :], ALU.mult, ALU.mult).then_inc(ln_nmr, 1)

            def low(j):
                v.wait_ge(ln_hi, j + 1)
                v.tensor_tensor(xl[:, j, :], TR2[j][:, :], xh[:, j, :], ALU.subtract).then_inc(ln_lo, 1)

            def gate(h, *which):
                tiles = slice(h * T // 2, (h + 1) * T // 2)
                wide = [P, T // 2, E]

                def over_e(t):
                    return t[:, tiles].unsqueeze(2).to_broadcast(wide)

                firsts = first[:, :].unsqueeze(1).to_broadcast(wide)
                for n in which:
                    if n == 0:
                        v.wait_ge(gate_mm, h + 1)
                        done = v.tensor_tensor(lg[:, tiles, :], GATE[:, 0:T // 2 * E].rearrange("p (t e) -> p t e", e=E),
                                               gb[:, :].unsqueeze(1).to_broadcast(wide), ALU.add)
                        done.then_inc(gate_step, 1)
                        continue
                    v.wait_ge(gate_step, GSTEPS * h + n)
                    if n == 1:
                        done = v.tensor_reduce(m1[:, tiles], lg[:, tiles, :], AX.X, ALU.max)
                    elif n == 2:
                        done = v.tensor_tensor(dl[:, tiles, :], lg[:, tiles, :], over_e(m1), ALU.subtract)
                    elif n == 3:
                        done = v.scalar_tensor_tensor(sc[:, tiles, :], dl[:, tiles, :], 0.0, firsts, ALU.is_equal, ALU.mult)
                    elif n in (4, 10):
                        done = v.tensor_reduce(ms[:, tiles], sc[:, tiles, :], AX.X, ALU.max)
                    elif n == 5:
                        done = v.tensor_tensor(top1[:, tiles, :], sc[:, tiles, :], over_e(ms), ALU.is_equal)
                    elif n == 6:
                        done = v.scalar_tensor_tensor(lg[:, tiles, :], top1[:, tiles, :], FAR, dl[:, tiles, :], ALU.mult, ALU.add)
                    elif n == 7:
                        done = v.tensor_reduce(m2[:, tiles], lg[:, tiles, :], AX.X, ALU.max)
                    elif n == 8:
                        done = v.tensor_tensor(eq[:, tiles, :], lg[:, tiles, :], over_e(m2), ALU.is_equal)
                    elif n == 9:
                        done = v.tensor_tensor(sc[:, tiles, :], eq[:, tiles, :], firsts, ALU.mult)
                    elif n == 11:
                        done = v.tensor_tensor(top2[:, tiles, :], sc[:, tiles, :], over_e(ms), ALU.is_equal)
                    elif n == 12:
                        v.wait_ge(gate_exp, h + 1)
                        done = v.tensor_reduce(den[:, tiles], ex[:, tiles, :], AX.X, ALU.add)
                    elif n == 13:
                        done = v.reciprocal(den[:, tiles], den[:, tiles])
                    elif n == 14:
                        done = v.tensor_tensor(pr[:, tiles, :], ex[:, tiles, 0:2], den[:, tiles].unsqueeze(2).to_broadcast([P, T // 2, 2]), ALU.mult)
                    elif n == 15:
                        done = v.tensor_tensor(top1[:, tiles, :], top1[:, tiles, :], pr[:, tiles, 0:1].to_broadcast(wide), ALU.mult)
                    elif n == 16:
                        done = v.tensor_tensor(top2[:, tiles, :], top2[:, tiles, :], pr[:, tiles, 1:2].to_broadcast(wide), ALU.mult)
                    else:
                        done = v.tensor_tensor(cw[:, tiles, :], top1[:, tiles, :], top2[:, tiles, :], ALU.add)
                    done.then_inc(gate_step, 1)

            v.wait_ge(pool_const, 1)
            add_proj(0)
            v.wait_ge(crow_mm, 1)
            v.tensor_tensor(xt[:, 0, :, :], xt[:, 0, :, :], by_batch(CROW), ALU.add).then_inc(crow_read, 1)
            v.wait_ge(crow_read, 1)
            statistics(0)
            shift(0)
            add_proj(1)
            statistics(1)
            shift(1)
            low(0)
            add_proj(2)
            low(1)
            statistics(2)
            v.wait_ge(gb_here, 16)
            gate(0, 0)
            shift(2)
            gate(0, 1, 2)
            add_proj(3)
            gate(0, 3, 4, 5, 6)
            statistics(3)
            gate(0, 7, 8, 9)
            shift(3)
            gate(0, 10, 11, 12, 13, 14, 15, 16, 17)
            low(2)

            def cwT_copy(h):
                v.wait_ge(cwT_mm, h + 1)
                v.tensor_copy(cwT[:, 2 * h:2 * h + 2, :], CWT[0:B * E, 256:512].rearrange("p (j q) -> p j q", j=2)).then_inc(cwT_done, 1)

            def add_b3(j):
                v.wait_ge(b3_mm, j + 1)
                if j == 0:
                    v.wait_ge(y_used, 1)
                v.tensor_tensor(xt[:, j, :, :], xt[:, j, :, :], by_batch(B3P[j]), ALU.add).then_inc(b3_added, 1)

            def step(c, k):
                item = (c, k)
                first_chunk = isinstance(c, int) and c == 0
                if first_chunk and k in (2, 5):
                    cwT_copy(k // 3)
                if real(item):
                    q = k % 4
                    v.wait_ge(r2_done, at(item))
                    wait(v, y_mm, at(item, -3))
                    v.tensor_copy(h2[:, q, :], r2[:, q, :]).then_inc(h2_done, 1)
                    if first_chunk and 2 <= k <= 4:
                        gate(1, *((0, 1, 2), (6, 7, 8, 9), (13, 14, 15))[k - 2])
                    if first_chunk and k in (3, 5):
                        add_b3(k - 3)
                    if k % 2 == 1:
                        v.wait_ge(h2_done, at(item))
                        v.tensor_tensor(l2[:, q, :], r2[:, q, :], h2[:, q, :], ALU.subtract).then_inc(l2_dve, 1)
                if first_chunk and k == 0:
                    low(3)
                if first_chunk and 2 <= k <= 4:
                    gate(1, *((3, 4, 5), (10, 11, 12), (16, 17))[k - 2])
                if first_chunk and k in (4, 5):
                    add_b3(2 * k - 7)
                item = back(c, k, 2)
                if real(item):
                    chunk, e = item
                    v.wait_ge(y_mm, at(item))
                    wait(v, y_used, at(item, 0))
                    for t in range(B):
                        y = xt[:, chunk, t, :]
                        done = v.scalar_tensor_tensor(y, Y[e % 2][:, t * D:(t + 1) * D], cw[:, chunk * B + t, e:e + 1], y, ALU.mult, ALU.add)
                    done.then_inc(y_used, 1)
                if first_chunk and k == 5:
                    v.wait_ge(b3_added, J)

            over_items(v, step, 2)

        @block.tensor
        def _(pe):
            pe.wait_ge(ident_done, 2)
            for b in range(B):
                pe.wait_ge(x_here[b], 16)
                for j in range(J):
                    done = pe.transpose(XT[b][:, j * P:(j + 1) * P], xt[:, j, b, :], ident[:, :])
                done.then_inc(xT_mm, 1)
                if b == 0:
                    pe.wait_ge(wdi_here, 32)
                    pe.wait_ge(centre_done, 1)
                    pe.matmul(WCEN[:, 0:2 * N], centre[:, :], wdi[:, 0, :, :], start=True, stop=True).then_inc(wcen_mm, 1)
            pe.wait_ge(rows_here, 16 * 8)
            pe.transpose(MISC[:, 0:ROWS], rows[:, :], ident[0:ROWS, 0:ROWS]).then_inc(rowsT_mm, 1)
            pe.wait_ge(wcen_done, 1)
            pe.wait_ge(xT_done, B)
            for kind, z, s in ((0, ZD, zd_mm), (1, ZI, zi_mm)):
                for b in range(B):
                    done = pe.matmul(z[b * N:(b + 1) * N, :], wcen[:, kind, :], xT[:, b, :], start=True, stop=True)
                done.then_inc(s, 1)
            pe.wait_ge(rexp_done, 1)
            for j in range(J):
                done = pe.transpose(RB[:, j * P:(j + 1) * P], rexp[:, j, :, :], ident[:, :])
            done.then_inc(rb_mm, 1)
            pe.wait_ge(cols_done, 1)
            pe.wait_ge(wos_here, 32)
            pe.transpose(MISC[:, 64:64 + 2 * N], wos0[:, :], ident[0:2 * N, 0:2 * N]).then_inc(wosT_mm, 1)
            pe.wait_ge(wosT_done, 1)
            for w in range(2):
                pe.matmul(COMP[:, w * 2 * P:(w + 1) * 2 * P], wosT[:, w, :, :], wdi1[:, :, :, :], start=True, stop=True)
            for kind in range(2):
                done = pe.matmul(MISC[:, 128 + kind:129 + kind], wdi1[:, kind, :, :], bsum0[:, :], start=True, stop=True)
            done.then_inc(comp_mm, 1)
            pe.wait_ge(zi_done, 1)
            pe.wait_ge(comp_done, 1)
            for i, h in enumerate(HALVES):
                pe.wait_ge(scanned, i + 1)
                if i == 1:
                    for kind in range(2):
                        done = pe.matmul(MISC[:, 132 + kind:133 + kind], comp[:, 1, kind, :], hs[:, 0, S - 1:S], start=True, stop=True)
                    done.then_inc(bias_mm, 1)
                for kind, z, s in ((0, ZD, zd_mm), (1, ZI, zi_mm)):
                    pe.matmul(z[:, h], comp[:, 0, kind, :], hs[:, 0, h], start=True, stop=True).then_inc(s, 1)
            pe.wait_ge(bobs_here, 32)
            pe.wait_ge(blocks_done, 2)
            pe.wait_ge(bias_done, 1)
            for b in range(B):
                pe.matmul(CROW[:, b * D:(b + 1) * D], ones[:, :], bobs[:, :], start=b == 0, stop=False, skip_group_check=True)

            def hidden(j):
                pe.matmul(PROJ[j][:, :], hs[:, 1, j * P:(j + 1) * P], wo1[:, :, :], start=True, stop=True).then_inc(proj_mm, 1)

            pe.wait_ge(scanned, 3)
            hidden(0)
            pe.wait_ge(last_done, 1)
            pe.matmul(CROW[:, :], last[:, :], ws1[:, :, :], start=False, stop=True, skip_group_check=True).then_inc(crow_mm, 1)
            hidden(1)
            hidden(2)
            hidden(3)

            def transposes(j):
                pe.wait_ge(norm_act, j + 1)
                pe.wait_ge(norm_pool, j + 1)
                if j == 1:
                    pe.wait_ge(crow_done, 1)
                if j >= 2:
                    pe.wait_ge(ln_lo, j)
                for t in range(B):
                    done = pe.transpose(TR2[j][:, t * P:(t + 1) * P], xn[:, j % 2, t, :], ident[:, :])
                done.then_inc(ln_tr, 1)

            def gates(h):
                pe.wait_ge(ln_lo, 2 * h + 2)
                if h == 1:
                    pe.wait_ge(gate_step, 1)
                    pe.wait_ge(cwT_done, 1)
                for n in range(T // 2):
                    j, to, tok = 2 * h + n // B, GATE[:, n * E:(n + 1) * E], slice(n % B * P, (n % B + 1) * P)
                    pe.matmul(to, xh[:, j, tok], gw16[:, 0, :], start=True, stop=False)
                    pe.matmul(to, xl[:, j, tok], gw16[:, 0, :], start=False, stop=False)
                    done = pe.matmul(to, xh[:, j, tok], gw16[:, 1, :], start=False, stop=True)
                done.then_inc(gate_mm, 1)

            def weights_transposed(h):
                pe.wait_ge(gate_step, GSTEPS * (h + 1))
                for n in range(2):
                    j = 2 * h + n
                    done = pe.transpose(CWT[0:B * E, 256 + n * P:256 + (n + 1) * P], cw[:, j * B:(j + 1) * B, :], ident[:, :])
                done.then_inc(cwT_mm, 1)

            def b3_term(j):
                pe.wait_ge(cwT_done, j // 2 + 1)
                if j == 0:
                    pe.wait_ge(blocks_done, 3)
                    pe.wait_ge(ln_lo, J)
                elif j < 3:
                    pe.wait_ge(b3_added, j)
                pe.matmul(B3P[j][:, :], cwT[:, j, :], b3d[:, :, :], start=True, stop=True).then_inc(b3_mm, 1)

            transposes(0)
            transposes(1)
            pe.wait_ge(wl_done, 3)

            def step(c, k):
                item = (c, k)
                first_chunk = isinstance(c, int) and c == 0
                if real(item):
                    if k == 0:
                        wait(pe, ln_lo, c + 1)
                    wait(pe, h1_done, at(item, -1))
                    z = Z1[k % 2][:, :]
                    pe.matmul(z, wh[:, 0, k, :], xh[:, c, :], start=True, stop=False)
                    pe.matmul(z, wl[:, 0, k, :], xh[:, c, :], start=False, stop=False)
                    pe.matmul(z, wh[:, 0, k, :], xl[:, c, :], start=False, stop=True).then_inc(z1_mm, 1)
                item = back(c, k, 2)
                if real(item):
                    e, q = item[1], item[1] % 4
                    if first_chunk:
                        wait(pe, ln_stat, min(k, 4))
                    wait(pe, r2_done, at(item, -1))
                    pe.wait_ge(h1_done, at(item))
                    z = Z2[e % 2][:, :]
                    pe.matmul(z, wh[:, 1, e, :], h1[:, q, :], start=True, stop=False)
                    pe.matmul(z, wl[:, 1, e, :], h1[:, q, :], start=False, stop=False)
                    pe.wait_ge(l1_done, at(item))
                    pe.matmul(z, wh[:, 1, e, :], l1[:, q, :], start=False, stop=True).then_inc(z2_mm, 1)
                item = back(c, k, 4)
                if real(item):
                    e, q = item[1], item[1] % 4
                    wait(pe, y_used, at(item, -1))
                    pe.wait_ge(h2_done, at(item))
                    wait_l2(pe, item)
                    for t in range(B):
                        y, tok = Y[e % 2][:, t * D:(t + 1) * D], slice(t * P, (t + 1) * P)
                        pe.matmul(y, h2[:, q, tok], wh[:, 2, e, :], start=True, stop=False)
                        pe.matmul(y, h2[:, q, tok], wl[:, 2, e, :], start=False, stop=False)
                        done = pe.matmul(y, l2[:, q, tok], wh[:, 2, e, :], start=False, stop=True)
                    done.then_inc(y_mm, 1)
                if first_chunk and k == 1:
                    gates(0)
                if first_chunk and k in (2, 3):
                    transposes(k)
                if first_chunk and k == 3:
                    weights_transposed(0)
                if first_chunk and k == 4:
                    gates(1)
                if first_chunk and k in (5, 6):
                    b3_term(k - 5)
                if first_chunk and k == 6:
                    weights_transposed(1)
                if first_chunk and k == 7:
                    b3_term(2)
                    b3_term(3)

            over_items(pe, step, 4)


_INS = ["L0_attn_shot_embeddings", "L0_attn_Wd", "L0_attn_bd", "L0_attn_Wi", "L0_attn_bi", "L0_attn_A_log", "L0_attn_Wo",
        "L0_attn_bo", "L0_attn_Ws", "L0_attn_bs", "L0_ffn_gate_w", "L0_ffn_gate_b", "L0_ffn_w1", "L0_ffn_b1", "L0_ffn_w2",
        "L0_ffn_b2", "L0_ffn_w3", "L0_ffn_b3"]


def kernel(**inputs):
    import numpy as _np
    import concourse.bacc as _bacc
    from concourse.bass_utils import run_bass_kernel_spmd as _run

    nc = _bacc.Bacc("TRN2", target_bir_lowering=False, num_devices=1)
    arrays, args = {}, []
    for name in _INS:
        a = _np.ascontiguousarray(inputs[name])
        arrays[f"in_{name}"] = a
        args.append(nc.dram_tensor(f"in_{name}", a.shape, mybir.dt.from_np(a.dtype), kind="ExternalInput").ap())
    args.append(nc.dram_tensor("result", [B, S, D], F32, kind="ExternalOutput").ap())
    program(nc, *args)
    r = _run(nc, [arrays], core_ids=[0])
    return r.results[0]["result"]
```

```python
from contextlib import ExitStack

import concourse.bass as bass
from concourse import mybir

F32 = mybir.dt.float32
F16 = mybir.dt.float16
ALU = mybir.AluOpType
ACT = mybir.ActivationFunctionType
AX = mybir.AxisListType

P = 128
B, S, D = 4, 512, 128
N = 32
L = 2
E = 8
J = S // P
ITEMS = J * E
EPS = 1e-5
WARM = (9, 8)
AHEAD = 2
LAG2, LAG3 = 2, 4
DEPTH = 4
NORM_ACT, NORM_POOL, NORM_VECTOR = ((0,), (0, 1)), ((3,), (2, 3)), (1, 2)
GROUPS = ((0, 1), (1, J))
POOL_L2 = [(0, 2, 4, 5, 6, 7), (0, 1, 2, 4, 6), (0, 2, 4, 6)]
GSTEPS = 18
CAP = 20.0
FAR = -1e30

R_BO, R_BS, R_BD, R_BI, R_A = 0, L, 2 * L, 3 * L, 4 * L
ROWS_SCAN = 5 * L
R_B1, R_B2, R_GW = ROWS_SCAN, ROWS_SCAN + E, ROWS_SCAN + 2 * E
ROWS_FFN = 3 * E
ROWS = ROWS_SCAN + ROWS_FFN


def program(nc, x_in, Wd, bd, Wi, bi, A_log, Wo, bo, Ws, bs, gate_w, gate_b, w1, b1, w2, b2, w3, b3, out):
    with ExitStack() as ctx:
        def sb(name, shape, dt=F32):
            return ctx.enter_context(nc.sbuf_tensor(name, shape, dt))

        def sem(name):
            return ctx.enter_context(nc.semaphore(name))

        bank = [ctx.enter_context(nc.psum_tensor(f"bank{i}", [P, 512], F32)) for i in range(8)]
        ZD, ZI = bank[0], bank[1]
        Z2H = [bank[0:2], [bank[7], bank[2]]]
        XT = bank[2:6]
        RB = bank[2]
        PROJ = [*bank[3:6], bank[2]]
        IDLE = bank[5]
        MISC = bank[6]
        WCEN, COMP = bank[7], bank[7]
        TR2 = [bank[7], bank[6], bank[6], bank[7]]
        GATE, CWT, B3P = bank[7], bank[7], [bank[6], bank[6], bank[7], bank[6]]
        Z1, Z2, Y = bank[0:2], bank[3:5], [bank[5], bank[2]]

        ident = sb("ident", [P, P])
        centre = sb("centre", [P, P])
        of_batch = sb("of_batch", [P, B])
        of_tile = sb("of_tile", [B * E, B])
        eps = sb("eps", [P, 1])
        first = sb("first", [P, E])
        rows = sb("rows", [ROWS_SCAN, P])
        rows_ffn = sb("rows_ffn", [ROWS_FFN, P])
        cols = sb("cols", [P, ROWS])
        wdi = sb("wdi", [P, L, 2, N])
        wcen = sb("wcen", [P, 2, N])
        wos0 = sb("wos0", [2 * N, D])
        wosT = sb("wosT", [P, 2, B, N])
        wdi1 = sb("wdi1", [P, 2, B, N])
        bobs = sb("bobs", [P, 2, D])
        bsum1 = sb("bsum1", [P, D])
        bsum0 = sb("bsum0", [P, 1])
        comp = sb("comp", [P, 2, 2, P])
        wos1 = sb("wos1", [P, 2, D])
        wo1 = sb("wo1", [P, B, D])
        ws1 = sb("ws1", [P, B, D])
        const2 = sb("const2", [P, 2])
        bias2 = sb("bias2", [P, 2])
        spa = sb("spa", [P, 4, L])
        nspa = sb("nspa", [P, L])
        gw16 = sb("gw16", [P, 2, E], F16)
        gb = sb("gb", [P, E])
        b3r = sb("b3r", [B * E, D])
        b3d = sb("b3d", [B * E, B, D])
        b3h = sb("b3h", [B * E, B, D], F16)
        b3l = sb("b3l", [B * E, B, D], F16)
        xt = sb("xt", [P, J, B, D])
        stats = sb("stats", [P, B, J, 6])
        var = sb("var", [P, 4, B, J])
        lnv1 = sb("lnv1", [P, B, J])
        rstd1 = sb("rstd1", [P, B, J])
        rexp = sb("rexp", [P, J, B, N])
        rb = sb("rb", [P, S])
        xT = sb("xT", [P, B, S])
        stats2 = sb("stats2", [P, J, B, 6])
        mv = sb("mv", [P, J, B, 2])
        lnv = sb("lnv", [P, J, B])
        rstd = sb("rstd", [P, J, B])
        nmr = sb("nmr", [P, J, B])
        xn = sb("xn", [P, 2, B, D])
        zd = sb("zd", [P, S])
        zi = sb("zi", [P, S])
        lowz = sb("lowz", [P, S])
        expz = sb("expz", [P, S])
        logz = sb("logz", [P, S])
        delta = sb("delta", [P, S])
        decay = sb("decay", [P, S])
        drive = sb("drive", [P, S])
        hs = sb("hs", [P, L, S])
        last = sb("last", [P, P])
        wf = sb("wf", [P, 3, E, D])
        wh = sb("wh", [P, 3, E, D], F16)
        wl = sb("wl", [P, 3, E, D], F16)
        xh = sb("xh", [P, J, 512], F16)
        xl = sb("xl", [P, J, 512], F16)
        r1 = sb("r1", [P, DEPTH, 512])
        h1 = sb("h1", [P, DEPTH, 512], F16)
        l1 = sb("l1", [P, DEPTH, 512], F16)
        r2 = sb("r2", [P, DEPTH, 512])
        h2 = sb("h2", [P, DEPTH, 512], F16)
        l2 = sb("l2", [P, DEPTH, 512], F16)
        T = J * B
        lg = sb("lg", [P, T, E])
        dl = sb("dl", [P, T, E])
        m1 = sb("m1", [P, T])
        m2 = sb("m2", [P, T])
        eq = sb("eq", [P, T, E])
        sc = sb("sc", [P, T, E])
        ms = sb("ms", [P, T])
        top1 = sb("top1", [P, T, E])
        top2 = sb("top2", [P, T, E])
        ex = sb("ex", [P, T, E])
        den = sb("den", [P, T])
        pr = sb("pr", [P, T, 2])
        cw = sb("cw", [P, T, E])
        cwTh = sb("cwTh", [B * E, J, P], F16)
        cwTl = sb("cwTl", [B * E, J, P], F16)

        x_here = [sem(f"x_here{b}") for b in range(B)]
        w_here = [sem(f"w_here{i}") for i in range(3)]
        rows_here, ffn_rows_here, wdi_here, wos_here, bobs_here, wos1_here, gb_here, b3_here = (
            sem(n) for n in ("rows_here", "ffn_rows_here", "wdi_here", "wos_here", "bobs_here", "wos1_here", "gb_here", "b3_here"))
        ident_done, constants_done, centre_done, masks_done, blocks_done = (
            sem(n) for n in ("ident_done", "constants_done", "centre_done", "masks_done", "blocks_done"))
        rowsT_mm, ffn_rowsT_mm, cols_done, ffn_cols_done, wcen_mm, wcen_done, wosT_mm, wosT_done, comp_mm, comp_done = (
            sem(n) for n in ("rowsT_mm", "ffn_rowsT_mm", "cols_done", "ffn_cols_done", "wcen_mm", "wcen_done", "wosT_mm", "wosT_done", "comp_mm", "comp_done"))
        xT_mm, xT_done, var_done, lnv1_done, rstd1_done, rexp_done, rb_mm, rb_done = (
            sem(n) for n in ("xT_mm", "xT_done", "var_done", "lnv1_done", "rstd1_done", "rexp_done", "rb_mm", "rb_done"))
        a_low, a_act, a_done = sem("a_low"), sem("a_act"), sem("a_done")
        zd_mm, zi_mm, zd_done, zi_done, z_low, z_exp, z_log, z_delta, z_decay, z_drive, scanned = (
            sem(n) for n in ("zd_mm", "zi_mm", "zd_done", "zi_done", "z_low", "z_exp", "z_log", "z_delta", "z_decay",
                             "z_drive", "scanned"))
        bsum_done, const_done, bias_mm, bias_done = (sem(n) for n in ("bsum_done", "const_done", "bias_mm", "bias_done"))
        biased, last_done, proj_mm = sem("biased"), sem("last_done"), sem("proj_mm")
        ln_stat, ln_log, ln_rstd, ln_nmr, norm_act, norm_pool, norm_vector, ln_tr, ln_hi, ln_lo = (
            sem(n) for n in ("ln_stat", "ln_log", "ln_rstd", "ln_nmr", "norm_act", "norm_pool", "norm_vector", "ln_tr", "ln_hi", "ln_lo"))
        gate_mm, gate_step, gate_exp, cwT_mm, cwT_done, b3_mm, b3_added = (
            sem(n) for n in ("gate_mm", "gate_step", "gate_exp", "cwT_mm", "cwT_done", "b3_mm", "b3_added"))
        wh_done, wl_done = sem("wh_done"), sem("wl_done")
        dve = sem("dve")
        z1_mm, z2_mm, y_mm = sem("z1_mm"), sem("z2_mm"), sem("y_mm")
        r1_done, h1_done, l1_done, r2_done, h2_done = (
            sem(n) for n in ("r1_done", "h1_done", "l1_done", "r2_done", "h2_done"))
        l2_pool, l2_dve, y_used = sem("l2_pool"), sem("l2_dve"), sem("y_used")
        b3_split, half_done, stored = sem("b3_split"), sem("half_done"), sem("stored")

        block = ctx.enter_context(nc.Block())

        def at(item, plus=1):
            c, k = item
            return c * E + (k + plus)

        def back(c, k, lag):
            return (c, k - lag) if k >= lag else (c - 1, k - lag + E)

        def real(item):
            c, k = item
            return not isinstance(c, int) or 0 <= c * E + k < ITEMS

        def wait(eng, s, value):
            if not isinstance(value, int) or value > 0:
                eng.wait_ge(s, value)

        def l2_on_pool(c):
            return POOL_L2[c] if isinstance(c, int) and c < AHEAD else POOL_L2[AHEAD]

        def wait_l2(eng, item, plus=1):
            c, k = item[0], item[1] + plus - 1
            if k < 0:
                c, k = c - 1, k + E
            if isinstance(c, int) and c < 0:
                return
            mine, usual = l2_on_pool(c), len(POOL_L2[AHEAD])
            earlier = POOL_L2[:c] if isinstance(c, int) and c < AHEAD else POOL_L2[:AHEAD]
            more = sum(len(e) - usual for e in earlier)
            on_pool = sum(e <= k for e in mine)
            wait(eng, l2_pool, c * usual + (more + on_pool))
            wait(eng, l2_dve, c * (E - usual) + (k + 1 - on_pool - more))

        def over_items(eng, step, lag):
            for c in range(AHEAD):
                for k in range(E):
                    step(c, k)
            with eng.Fori(AHEAD, J) as c:
                for k in range(E):
                    step(c, k)
            for k in range(lag):
                step(J, k)

        def place(c, k):
            return c * E + k if isinstance(c, int) and c < AHEAD else None

        HALVES = [slice(0, S // 2), slice(S // 2, S)]

        def by_batch(psum):
            return psum[:, :].rearrange("p (b d) -> p b d", b=B)

        @block.sync
        def _(sp):
            for b in range(B):
                sp.dma_start(xt[:, :, b, :], x_in[b].rearrange("(j p) d -> p j d", p=P)).then_inc(x_here[b], 16)
            for r, v in ((R_BD, bd), (R_BI, bi), (R_A, A_log)):
                sp.dma_start(rows[r:r + L, :].rearrange("l (b n) -> l b n", b=B),
                             v.unsqueeze(1).to_broadcast([L, B, N])).then_inc(rows_here, 16)
            for r, v in ((R_BO, bo), (R_BS, bs)):
                sp.dma_start(rows[r:r + L, :], v).then_inc(rows_here, 16)
            for i, w in enumerate((w1, w2, w3)):
                sp.dma_start(wf[:, i, :, :], w.rearrange("e d o -> d e o")).then_inc(w_here[i], 16)
            for c in range(J - 1):
                sp.wait_ge(y_used, (c + 1) * E)
                sp.dma_start(out[:, c * P:(c + 1) * P, :].rearrange("b p d -> p b d"), xt[:, c, :, :]).then_inc(stored, 16)
            for n, (s, value) in enumerate(((half_done, 1), (y_used, ITEMS))):
                sp.wait_ge(s, value)
                half = slice(n * B // 2, (n + 1) * B // 2)
                sp.dma_start(out[half, S - P:S, :].rearrange("b p d -> p b d"), xt[:, J - 1, half, :]).then_inc(stored, 16)
            sp.wait_ge(stored, 16 * (J - 1 + 2))

        @block.gpsimd
        def _(pool):
            pool.memset(ident[:, :], 0.0).then_inc(ident_done, 1)
            pool.wait_ge(ident_done, 1)
            pool.affine_select(out=ident[:, :], in_=ident[:, :], compare_op=ALU.not_equal, fill=1.0, base=0,
                               pattern=[[-1, P]], channel_multiplier=1).then_inc(ident_done, 1)
            for w, v in enumerate((Wo, Ws)):
                pool.dma_start(wos1[:, w, :], v[1].partition_broadcast(B)).then_inc(wos1_here, 16)
            for i, v in enumerate((bo, bs)):
                pool.dma_start(bobs[:, i, :], v[1].partition_broadcast(P)).then_inc(bobs_here, 16)
            for r, v in ((R_B1, b1), (R_B2, b2), (R_GW, gate_w)):
                pool.dma_start(rows_ffn[r - ROWS_SCAN:r - ROWS_SCAN + E, :], v).then_inc(ffn_rows_here, 16)
            pool.dma_start(b3r[:, :], b3.partition_broadcast(B)).then_inc(b3_here, 16)
            pool.dma_start(gb[:, :], gate_b.partition_broadcast(P)).then_inc(gb_here, 16)
            pool.wait_ge(masks_done, 2)
            pool.wait_ge(wos1_here, 32)
            for w, to in enumerate((wo1, ws1)):
                pool.tensor_tensor(to[:, :, :], wos1[:, w, :].unsqueeze(1).to_broadcast([P, B, D]),
                                   of_batch[:, :].unsqueeze(2).to_broadcast([P, B, D]), ALU.mult).then_inc(blocks_done, 1)
            pool.wait_ge(b3_here, 16)
            pool.wait_ge(blocks_done, 2)
            pool.tensor_tensor(b3d[:, :, :], b3r[:, :].unsqueeze(1).to_broadcast([B * E, B, D]),
                               of_tile[:, :].unsqueeze(2).to_broadcast([B * E, B, D]), ALU.mult).then_inc(blocks_done, 1)
            pool.wait_ge(bobs_here, 32)
            pool.tensor_tensor(bsum1[:, :], bobs[:, 0, :], bobs[:, 1, :], ALU.add).then_inc(biased, 1)
            pool.wait_ge(biased, 1)
            pool.wait_ge(xT_mm, B)
            pool.wait_ge(var_done, 1)
            for j in range(J):
                pool.tensor_tensor(xt[:, j, :, :], xt[:, j, :, :], bsum1[:, :].unsqueeze(1).to_broadcast([P, B, D]), ALU.add).then_inc(biased, 1)

            def low_weights(i):
                pool.wait_ge(wh_done, i + 1)
                pool.tensor_tensor(wl[:, i, :, :], wf[:, i, :, :], wh[:, i, :, :], ALU.subtract).then_inc(wl_done, 1)

            low_weights(0)
            low_weights(1)

            def normalise(j):
                pool.wait_ge(ln_nmr, j + 1)
                if j >= 2:
                    pool.wait_ge(ln_tr, j - 1)
                for t in NORM_POOL[min(j, 1)]:
                    done = pool.tensor_scalar(xn[:, j % 2, t, :], xt[:, j, t, :], rstd[:, j, t:t + 1], nmr[:, j, t:t + 1],
                                              ALU.mult, ALU.add)
                done.then_inc(norm_pool, 1)

            normalise(0)
            low_weights(2)
            normalise(1)

            def step(c, k):
                item = (c, k)
                if place(c, k) == 5:
                    normalise(3)
                if real(item):
                    pool.wait_ge(r1_done, at(item))
                    pool.wait_ge(h1_done, at(item))
                    wait(pool, z2_mm, at(item, 1 - DEPTH))
                    pool.tensor_tensor(l1[:, k % DEPTH, :], r1[:, k % DEPTH, :], h1[:, k % DEPTH, :], ALU.subtract).then_inc(l1_done, 1)
                if place(c, k) == 3:
                    normalise(2)
                item = back(c, k, LAG2)
                if real(item) and item[1] in l2_on_pool(item[0]):
                    q = item[1] % DEPTH
                    pool.wait_ge(h2_done, at(item))
                    wait(pool, y_mm, at(item, 1 - DEPTH))
                    pool.tensor_tensor(l2[:, q, :], r2[:, q, :], h2[:, q, :], ALU.subtract).then_inc(l2_pool, 1)

            over_items(pool, step, LAG2)

        @block.scalar
        def _(act):
            act.dma_start(wdi[:, :, 0, :], Wd.rearrange("l d n -> d l n")).then_inc(wdi_here, 16)
            act.dma_start(wdi[:, :, 1, :], Wi.rearrange("l d n -> d l n")).then_inc(wdi_here, 16)
            act.preload_act_table_set("natural_log_exp_and_others")
            act.dma_start(wos0[0:N, :], Wo[0]).then_inc(wos_here, 16)
            act.dma_start(wos0[N:2 * N, :], Ws[0]).then_inc(wos_here, 16)

            for b in range(B):
                act.wait_ge(xT_mm, b + 1)
                act.activation(xT[:, b, :], XT[b][:, :], ACT.Copy).then_inc(xT_done, 1)
            act.wait_ge(var_done, 4)
            act.activation(lnv1[:, :, :], var[:, 3, :, :], ACT.Ln, bias=eps[:, :], scale=1.0 / D).then_inc(lnv1_done, 1)
            act.wait_ge(lnv1_done, 1)
            act.activation(rstd1[:, :, :], lnv1[:, :, :], ACT.Exp, scale=-0.5).then_inc(rstd1_done, 1)
            act.wait_ge(rb_mm, 1)
            for h in HALVES:
                act.activation(rb[:, h], RB[:, h], ACT.Copy).then_inc(rb_done, 1)

            for l in range(L):
                if l == 0:
                    act.wait_ge(comp_mm, 1)
                    act.wait_ge(masks_done, 1)
                    for b in range(B):
                        blk = slice(b * N, (b + 1) * N)
                        done = act.activation(comp[:, :, :, blk], COMP[:, :].rearrange("p (w k m) -> p w k m", w=2, k=2)[:, :, :, blk],
                                              ACT.Copy, scale=of_batch[:, b:b + 1])
                    done.then_inc(comp_done, 1)
                for i, h in enumerate(HALVES):
                    n = 2 * l + i + 1
                    act.wait_ge(z_low, n)
                    act.activation(expz[:, h], lowz[:, h], ACT.Exp).then_inc(z_exp, 1)
                    if n == 1:
                        act.wait_ge(a_low, 1)
                        act.activation(spa[:, 1, :], spa[:, 0, :], ACT.Exp).then_inc(a_act, 1)
                    act.wait_ge(z_exp, n)
                    act.activation(logz[:, h], expz[:, h], ACT.Ln, bias=1.0).then_inc(z_log, 1)
                    if n == 1:
                        act.wait_ge(a_act, 1)
                        act.activation(spa[:, 2, :], spa[:, 1, :], ACT.Ln, bias=1.0).then_inc(a_act, 1)
                if l == 0:
                    act.wait_ge(a_done, 1)
                for i, h in enumerate(HALVES):
                    act.wait_ge(z_delta, 2 * l + i + 1)
                    act.activation(decay[:, h], delta[:, h], ACT.Exp, scale=nspa[:, l:l + 1]).then_inc(z_decay, 1)
                for i in ((0, 1), (2,))[l]:
                    act.wait_ge(w_here[i], 16)
                    act.activation(wh[:, i, :, :], wf[:, i, :, :], ACT.Copy).then_inc(wh_done, 1)

            act.wait_ge(blocks_done, 3)
            act.activation(b3h[:, :, :], b3d[:, :, :], ACT.Copy).then_inc(b3_split, 1)

            def rstd_of(j):
                act.wait_ge(ln_stat, j + 1)
                act.activation(lnv[:, j, :], mv[:, j, :, 1], ACT.Ln, bias=eps[:, :]).then_inc(ln_log, 1)
                act.wait_ge(ln_log, j + 1)
                act.activation(rstd[:, j, :], lnv[:, j, :], ACT.Exp, scale=-0.5).then_inc(ln_rstd, 1)

            def normalise(j):
                act.wait_ge(ln_nmr, j + 1)
                if j >= 2:
                    act.wait_ge(ln_tr, j - 1)
                for t in NORM_ACT[min(j, 1)]:
                    done = act.activation(xn[:, j % 2, t, :], xt[:, j, t, :], ACT.Identity, bias=nmr[:, j, t:t + 1],
                                          scale=rstd[:, j, t:t + 1])
                done.then_inc(norm_act, 1)

            def high(j):
                act.wait_ge(ln_tr, j + 1)
                act.activation(xh[:, j, :], TR2[j][:, :], ACT.Copy).then_inc(ln_hi, 1)

            def gate_exps(h):
                tiles = slice(B * GROUPS[h][0], B * GROUPS[h][1])
                act.wait_ge(gate_step, GSTEPS * h + 3)
                act.activation(ex[:, tiles, :], dl[:, tiles, :], ACT.Exp).then_inc(gate_exp, 1)

            rstd_of(0)
            normalise(0)
            high(0)
            rstd_of(1)
            meanwhile = {0: [(normalise, 1)], 1: [(gate_exps, 0)], 2: [(high, 1), (rstd_of, 2)], 3: [(normalise, 2)], 4: [(rstd_of, 3)],
                         5: [(normalise, 3), (high, 2)], 6: [(high, 3)], 9: [(gate_exps, 1)]}

            def step(c, k):
                item = (c, k)
                if real(item):
                    act.wait_ge(z1_mm, at(item))
                    wait(act, l1_done, at(item, 1 - DEPTH))
                    bias = cols[:, R_B1 + k:R_B1 + k + 1]
                    act.activation(r1[:, k % DEPTH, :], Z1[k % 2][:, :], ACT.Relu, bias=bias).then_inc(r1_done, 1)
                    wait(act, z2_mm, at(item, 1 - DEPTH))
                    act.activation(h1[:, k % DEPTH, :], Z1[k % 2][:, :], ACT.Relu, bias=bias).then_inc(h1_done, 1)
                item = back(c, k, LAG2)
                if real(item):
                    e = item[1]
                    act.wait_ge(z2_mm, at(item))
                    wait_l2(act, item, 1 - DEPTH)
                    act.activation(r2[:, e % DEPTH, :], Z2[e % 2][:, :], ACT.Relu, bias=cols[:, R_B2 + e:R_B2 + e + 1]).then_inc(r2_done, 1)
                for work, j in meanwhile.get(place(c, k), []):
                    work(j)

            over_items(act, step, LAG2)

        @block.vector
        def _(v):
            steps = [0]

            def then(done):
                steps[0] += 1
                done.then_inc(dve, 1)
                v.wait_ge(dve, steps[0])

            v.memset(eps[:, :], EPS)
            for e in range(E):
                done = v.memset(first[:, e:e + 1], float(E - e))
            done.then_inc(constants_done, 1)
            v.wait_ge(ident_done, 2)
            v.tensor_scalar(centre[:, :], ident[:, :], -1.0 / D, None, ALU.add).then_inc(centre_done, 1)
            v.tensor_reduce(of_batch[:, :], ident[:, :].rearrange("p (b n) -> p b n", b=B), AX.X, ALU.add).then_inc(masks_done, 1)
            v.tensor_reduce(of_tile[:, :], ident[0:B * E, 0:B * E].rearrange("p (t e) -> p t e", t=B), AX.X, ALU.add).then_inc(masks_done, 1)

            for b in range(B):
                v.wait_ge(x_here[b], 16)
                for j in range(J):
                    done = v.bn_stats(stats[:, b, j, :], xt[:, j, b, :])
                if b == 1:
                    v.wait_ge(wcen_mm, 1)
                    v.tensor_copy(wcen[:, :, :], WCEN[:, 0:2 * N].rearrange("p (w n) -> p w n", w=2)).then_inc(wcen_done, 1)
            then(done)
            v.tensor_tensor(var[:, 0, :, :], stats[:, :, :, 2], stats[:, :, :, 5], ALU.add).then_inc(var_done, 1)
            v.tensor_tensor(var[:, 1, :, :], stats[:, :, :, 1], stats[:, :, :, 4], ALU.subtract).then_inc(var_done, 1)
            v.wait_ge(var_done, 2)
            v.tensor_tensor(var[:, 2, :, :], var[:, 1, :, :], var[:, 1, :, :], ALU.mult).then_inc(var_done, 1)
            v.wait_ge(var_done, 3)
            v.scalar_tensor_tensor(var[:, 3, :, :], var[:, 2, :, :], D / 4.0, var[:, 0, :, :], ALU.mult, ALU.add).then_inc(var_done, 1)
            v.tensor_copy(wdi1[:, :, :, :], wdi[:, 1, :, :].unsqueeze(2).to_broadcast([P, 2, B, N]))
            v.wait_ge(wosT_mm, 1)
            v.tensor_copy(wosT[:, :, :, :], MISC[:, 64:64 + 2 * N].rearrange("p (w n) -> p w n", w=2).unsqueeze(2).to_broadcast([P, 2, B, N])).then_inc(wosT_done, 1)
            v.wait_ge(rstd1_done, 1)
            v.tensor_copy(rexp[:, :, :, :], rstd1[:, :, :].rearrange("p b j -> p j b").unsqueeze(3).to_broadcast([P, J, B, N])).then_inc(rexp_done, 1)

            for l in range(L):
                if l == 0:
                    v.wait_ge(zd_mm, 1)
                    for i, h in enumerate(HALVES):
                        v.wait_ge(rb_done, i + 1)
                        v.tensor_tensor(zd[:, h], ZD[:, h], rb[:, h], ALU.mult).then_inc(zd_done, 1)
                    v.wait_ge(rowsT_mm, 1)
                    v.tensor_copy(cols[:, 0:ROWS_SCAN], MISC[:, 0:ROWS_SCAN]).then_inc(cols_done, 1)
                    zs, bias_d, bias_i = [(zd[:, h], zi[:, h]) for h in HALVES], cols[:, R_BD:R_BD + 1], cols[:, R_BI:R_BI + 1]
                    v.wait_ge(cols_done, 1)
                else:
                    zs, bias_d, bias_i = [(Z2H[i][0][:, h], Z2H[i][1][:, h]) for i, h in enumerate(HALVES)], bias2[:, 0:1], bias2[:, 1:2]
                    v.wait_ge(bias_done, 1)
                for i, h in enumerate(HALVES):
                    if l == 0:
                        v.wait_ge(zd_done, i + 1)
                    else:
                        v.wait_ge(zd_mm, i + 2)
                    v.tensor_scalar(lowz[:, h], zs[i][0], bias_d, CAP, ALU.add, ALU.min).then_inc(z_low, 1)
                if l == 0:
                    v.tensor_scalar(spa[:, 0, :], cols[:, R_A:R_A + L], CAP, None, ALU.min).then_inc(a_low, 1)
                    v.tensor_tensor(bsum0[:, :], cols[:, R_BO:R_BO + 1], cols[:, R_BS:R_BS + 1], ALU.add).then_inc(bsum_done, 1)
                    v.wait_ge(zi_mm, 1)
                    v.tensor_tensor(zi[:, :], ZI[:, :], rb[:, :], ALU.mult).then_inc(zi_done, 1)
                    v.wait_ge(a_act, 2)
                    then(v.tensor_tensor(spa[:, 3, :], cols[:, R_A:R_A + L], spa[:, 2, :], ALU.max))
                    v.tensor_scalar(nspa[:, :], spa[:, 3, :], -1.0, None, ALU.mult).then_inc(a_done, 1)
                    v.wait_ge(comp_mm, 2)
                    v.tensor_tensor(const2[:, :], MISC[:, 128:130], cols[:, R_BD + 1:R_BI + 2:L], ALU.add).then_inc(const_done, 1)
                    v.wait_ge(zi_done, 1)

                def scan(i):
                    h, n = HALVES[i], 2 * l + i + 1
                    v.wait_ge(z_drive, n)
                    v.wait_ge(z_decay, n)
                    if i == 1:
                        v.wait_ge(scanned, n - 1)
                    v.tensor_tensor_scan(hs[:, l, h], decay[:, h], drive[:, h],
                                         0.0 if i == 0 else hs[:, l, h.start - 1:h.start], ALU.mult, ALU.add).then_inc(scanned, 1)

                for i, h in enumerate(HALVES):
                    v.wait_ge(z_log, 2 * l + i + 1)
                    v.scalar_tensor_tensor(delta[:, h], zs[i][0], bias_d, logz[:, h], ALU.add, ALU.max).then_inc(z_delta, 1)
                    if i == 1:
                        scan(0)
                    if l == 0:
                        v.wait_ge(zi_done, 1)
                    else:
                        v.wait_ge(zi_mm, i + 2)
                    v.wait_ge(z_delta, 2 * l + i + 1)
                    v.scalar_tensor_tensor(drive[:, h], zs[i][1], bias_i, delta[:, h], ALU.add, ALU.mult).then_inc(z_drive, 1)
                if l == 1:
                    v.wait_ge(ffn_rowsT_mm, 1)
                    v.tensor_copy(cols[:, ROWS_SCAN:ROWS], MISC[:, 0:ROWS_FFN]).then_inc(ffn_cols_done, 1)
                scan(1)
                if l == 0:
                    v.wait_ge(const_done, 1)
                    v.wait_ge(bias_mm, 2)
                    v.tensor_tensor(bias2[:, :], MISC[:, 132:134], const2[:, :], ALU.add).then_inc(bias_done, 1)
            v.wait_ge(scanned, 2 * L)
            v.tensor_copy(last[:, :], hs[:, 1, S - 1:S].to_broadcast([P, P])).then_inc(last_done, 1)
            v.wait_ge(ffn_cols_done, 1)
            then(v.tensor_copy(gw16[:, 0, :], cols[:, R_GW:R_GW + E]))
            v.tensor_tensor(gw16[:, 1, :], cols[:, R_GW:R_GW + E], gw16[:, 0, :], ALU.subtract)
            v.wait_ge(b3_split, 1)
            v.tensor_tensor(b3l[:, :, :], b3d[:, :, :], b3h[:, :, :], ALU.subtract).then_inc(b3_split, 1)

            def add_proj(j):
                v.wait_ge(biased, j + 2)
                v.wait_ge(proj_mm, j + 1)
                then(v.tensor_tensor(xt[:, j, :, :], xt[:, j, :, :], by_batch(PROJ[j]), ALU.add))

            def low(j):
                v.wait_ge(ln_hi, j + 1)
                v.tensor_tensor(xl[:, j, :], TR2[j][:, :], xh[:, j, :], ALU.subtract).then_inc(ln_lo, 1)

            def weave(big, small):
                small = list(small)
                for work in big:
                    if small:
                        small.pop(0)()
                    work()
                for work in small:
                    work()

            def statistics(j, small=(), between=None):
                def moments(t):
                    done = v.bn_stats(stats2[:, j, t, :], xt[:, j, t, :])
                    if t == B - 1:
                        steps[0] += 1
                        done.then_inc(dve, 1)
                        if between:
                            between()
                        v.wait_ge(dve, steps[0])

                def aggregate(t):
                    done = v.bn_aggr(mv[:, j, t, :], stats2[:, j, t, :])
                    if t == B - 1:
                        done.then_inc(ln_stat, 1)

                weave([lambda t=t, f=f: f(t) for f in (moments, aggregate) for t in range(B)], small)

            def shift(j):
                v.wait_ge(ln_rstd, j + 1)
                v.wait_ge(ln_stat, j + 1)
                v.scalar_tensor_tensor(nmr[:, j, :], mv[:, j, :, 0], -1.0, rstd[:, j, :], ALU.mult, ALU.mult).then_inc(ln_nmr, 1)

            def gate_steps(h, which):
                return [lambda n=n: gate(h, n) for n in which]

            def gate(h, *which):
                tiles = slice(B * GROUPS[h][0], B * GROUPS[h][1])
                count = tiles.stop - tiles.start
                wide = [P, count, E]

                def over_e(t):
                    return t[:, tiles].unsqueeze(2).to_broadcast(wide)

                firsts = first[:, :].unsqueeze(1).to_broadcast(wide)
                for n in which:
                    if n == 0:
                        v.wait_ge(gate_mm, h + 1)
                        done = v.tensor_tensor(lg[:, tiles, :], GATE[:, 0:count * E].rearrange("p (t e) -> p t e", e=E),
                                               gb[:, :].unsqueeze(1).to_broadcast(wide), ALU.add)
                        done.then_inc(gate_step, 1)
                        continue
                    v.wait_ge(gate_step, GSTEPS * h + n)
                    if n == 1:
                        done = v.tensor_reduce(m1[:, tiles], lg[:, tiles, :], AX.X, ALU.max)
                    elif n == 2:
                        done = v.tensor_tensor(dl[:, tiles, :], lg[:, tiles, :], over_e(m1), ALU.subtract)
                    elif n == 3:
                        done = v.scalar_tensor_tensor(sc[:, tiles, :], dl[:, tiles, :], 0.0, firsts, ALU.is_equal, ALU.mult)
                    elif n in (4, 10):
                        done = v.tensor_reduce(ms[:, tiles], sc[:, tiles, :], AX.X, ALU.max)
                    elif n == 5:
                        done = v.tensor_tensor(top1[:, tiles, :], sc[:, tiles, :], over_e(ms), ALU.is_equal)
                    elif n == 6:
                        done = v.scalar_tensor_tensor(lg[:, tiles, :], top1[:, tiles, :], FAR, dl[:, tiles, :], ALU.mult, ALU.add)
                    elif n == 7:
                        done = v.tensor_reduce(m2[:, tiles], lg[:, tiles, :], AX.X, ALU.max)
                    elif n == 8:
                        done = v.tensor_tensor(eq[:, tiles, :], lg[:, tiles, :], over_e(m2), ALU.is_equal)
                    elif n == 9:
                        done = v.tensor_tensor(sc[:, tiles, :], eq[:, tiles, :], firsts, ALU.mult)
                    elif n == 11:
                        done = v.tensor_tensor(top2[:, tiles, :], sc[:, tiles, :], over_e(ms), ALU.is_equal)
                    elif n == 12:
                        v.wait_ge(gate_exp, h + 1)
                        done = v.tensor_reduce(den[:, tiles], ex[:, tiles, :], AX.X, ALU.add)
                    elif n == 13:
                        done = v.reciprocal(den[:, tiles], den[:, tiles])
                    elif n == 14:
                        done = v.tensor_tensor(pr[:, tiles, :], ex[:, tiles, 0:2], den[:, tiles].unsqueeze(2).to_broadcast([P, count, 2]), ALU.mult)
                    elif n == 15:
                        done = v.tensor_tensor(top1[:, tiles, :], top1[:, tiles, :], pr[:, tiles, 0:1].to_broadcast(wide), ALU.mult)
                    elif n == 16:
                        done = v.tensor_tensor(top2[:, tiles, :], top2[:, tiles, :], pr[:, tiles, 1:2].to_broadcast(wide), ALU.mult)
                    else:
                        done = v.tensor_tensor(cw[:, tiles, :], top1[:, tiles, :], top2[:, tiles, :], ALU.add)
                    done.then_inc(gate_step, 1)

            v.wait_ge(constants_done, 1)
            add_proj(0)
            statistics(0)
            shift(0)
            v.wait_ge(ln_nmr, 1)
            for t in NORM_VECTOR:
                done = v.tensor_scalar(xn[:, 0, t, :], xt[:, 0, t, :], rstd[:, 0, t:t + 1], nmr[:, 0, t:t + 1], ALU.mult, ALU.add)
            done.then_inc(norm_vector, 1)
            add_proj(1)
            statistics(1, between=lambda: low(0))
            shift(1)
            v.wait_ge(gb_here, 16)
            weave([lambda: add_proj(2), lambda: add_proj(3)], gate_steps(0, range(0, 2)))
            statistics(2, gate_steps(0, range(2, 10)))
            gate(0, 10)

            def cwT_copy(h):
                v.wait_ge(cwT_mm, h + 1)
                chunks = slice(*GROUPS[h])
                cwT = CWT[0:B * E, chunks.start * P:chunks.stop * P].rearrange("p (j q) -> p j q", q=P)
                then(v.tensor_copy(cwTh[:, chunks, :], cwT))
                v.tensor_tensor(cwTl[:, chunks, :], cwT, cwTh[:, chunks, :], ALU.subtract).then_inc(cwT_done, 1)

            def add_b3(j):
                v.wait_ge(b3_mm, j + 1)
                if j < 2:
                    v.wait_ge(y_used, (6, 10)[j])
                v.tensor_tensor(xt[:, j, :, :], xt[:, j, :, :], by_batch(B3P[j]), ALU.add).then_inc(b3_added, 1)

            def before_sums(i):
                if i == 0:
                    statistics(3, gate_steps(0, range(11, GSTEPS)))
                    shift(2)
                if i == 1:
                    low(1)

            def after_sums(i):
                if i in (2, 10):
                    cwT_copy(i // 10)
                if i == 2:
                    shift(3)
                if i in (3, 4):
                    low(i - 1)
                if i in (7, 11, 12, 13):
                    add_b3({7: 0, 11: 1, 12: 2, 13: 3}[i])

            def step(c, k):
                i = place(c, k)
                item = (c, k)
                if real(item):
                    q = k % DEPTH
                    v.wait_ge(r2_done, at(item))
                    wait(v, y_mm, at(item, 1 - DEPTH))
                    v.tensor_copy(h2[:, q, :], r2[:, q, :]).then_inc(h2_done, 1)
                if i is not None:
                    before_sums(i)
                item = back(c, k, LAG3 - LAG2)
                if real(item):
                    chunk, e = item
                    v.wait_ge(y_mm, at(item))
                    wait(v, y_used, at(item, 0))
                    if i in (2, 10):
                        v.wait_ge(gate_step, GSTEPS * (i // 10 + 1))
                    if i in (8, 12, E * AHEAD - 1):
                        v.wait_ge(b3_added, {8: 1, 12: 2}.get(i, J))

                    def weigh(t):
                        y = xt[:, chunk, t, :]
                        done = v.scalar_tensor_tensor(y, Y[e % 2][:, t * D:(t + 1) * D], cw[:, chunk * B + t, e:e + 1], y, ALU.mult, ALU.add)
                        if t == B - 1:
                            done.then_inc(y_used, 1)
                        elif t == B // 2 - 1 and isinstance(chunk, int) and chunk * E + e == ITEMS - 1:
                            done.then_inc(half_done, 1)

                    small = gate_steps(1, range(5 * (i - 6), min(5 * (i - 5), GSTEPS))) if i in (6, 7, 8, 9) else []
                    weave([lambda t=t: weigh(t) for t in range(B)], small)
                if real((c, k)) and k not in l2_on_pool(c):
                    v.wait_ge(h2_done, at((c, k)))
                    v.tensor_tensor(l2[:, k % DEPTH, :], r2[:, k % DEPTH, :], h2[:, k % DEPTH, :], ALU.subtract).then_inc(l2_dve, 1)
                if i is not None:
                    after_sums(i)

            over_items(v, step, LAG3 - LAG2)

        @block.tensor
        def _(pe):
            def keep_warm(n):
                for _ in range(n):
                    pe.matmul(IDLE[:, 0:P], ident[:, :], ident[:, :], start=True, stop=True)

            pe.wait_ge(ident_done, 2)
            for b in range(B):
                pe.wait_ge(x_here[b], 16)
                for j in range(J):
                    done = pe.transpose(XT[b][:, j * P:(j + 1) * P], xt[:, j, b, :], ident[:, :])
                done.then_inc(xT_mm, 1)
                if b == 0:
                    pe.wait_ge(wdi_here, 32)
                    pe.wait_ge(centre_done, 1)
                    pe.matmul(WCEN[:, 0:2 * N], centre[:, :], wdi[:, 0, :, :], start=True, stop=True).then_inc(wcen_mm, 1)
            pe.wait_ge(wos_here, 32)
            pe.transpose(MISC[:, 64:64 + 2 * N], wos0[:, :], ident[0:2 * N, 0:2 * N]).then_inc(wosT_mm, 1)
            pe.wait_ge(wcen_done, 1)
            pe.wait_ge(xT_done, B)
            for kind, z, z_mm in ((0, ZD, zd_mm), (1, ZI, zi_mm)):
                for b in range(B):
                    done = pe.matmul(z[b * N:(b + 1) * N, :], wcen[:, kind, :], xT[:, b, :], start=True, stop=True)
                done.then_inc(z_mm, 1)
                if kind == 0:
                    pe.wait_ge(rexp_done, 1)
                    for j in range(J):
                        done = pe.transpose(RB[:, j * P:(j + 1) * P], rexp[:, j, :, :], ident[:, :])
                    done.then_inc(rb_mm, 1)
                    pe.wait_ge(wosT_done, 1)
                    pe.wait_ge(rows_here, 16 * 5)
                    pe.transpose(MISC[:, 0:ROWS_SCAN], rows[:, :], ident[0:ROWS_SCAN, 0:ROWS_SCAN]).then_inc(rowsT_mm, 1)
                    for w in range(2):
                        done = pe.matmul(COMP[:, w * 2 * P:(w + 1) * 2 * P], wosT[:, w, :, :], wdi1[:, :, :, :], start=True, stop=True)
                    done.then_inc(comp_mm, 1)
            pe.wait_ge(cols_done, 1)
            pe.wait_ge(bsum_done, 1)
            for kind in range(2):
                done = pe.matmul(MISC[:, 128 + kind:129 + kind], wdi1[:, kind, :, :], bsum0[:, :], start=True, stop=True)
            done.then_inc(comp_mm, 1)
            keep_warm(WARM[0])
            pe.wait_ge(zi_done, 1)
            pe.wait_ge(comp_done, 1)
            pe.wait_ge(const_done, 1)

            def inputs(i, kind, z_mm):
                pe.matmul(Z2H[i][kind][:, HALVES[i]], comp[:, 0, kind, :], hs[:, 0, HALVES[i]], start=True, stop=True).then_inc(z_mm, 1)

            pe.wait_ge(scanned, 1)
            inputs(0, 0, zd_mm)
            pe.wait_ge(scanned, 2)
            for kind in range(2):
                pe.matmul(MISC[:, 132 + kind:133 + kind], comp[:, 1, kind, :], hs[:, 0, S - 1:S], start=True, stop=True).then_inc(bias_mm, 1)
            inputs(1, 0, zd_mm)
            inputs(0, 1, zi_mm)
            inputs(1, 1, zi_mm)
            pe.wait_ge(ffn_rows_here, 16 * 3)
            pe.wait_ge(bias_done, 1)
            pe.transpose(MISC[:, 0:ROWS_FFN], rows_ffn[:, :], ident[0:ROWS_FFN, 0:ROWS_FFN]).then_inc(ffn_rowsT_mm, 1)
            keep_warm(WARM[1])
            pe.wait_ge(blocks_done, 2)
            pe.wait_ge(scanned, 3)

            def proj_hidden(j):
                if j == J // 2:
                    pe.wait_ge(scanned, 4)
                pe.matmul(PROJ[j][:, :], hs[:, 1, j * P:(j + 1) * P], wo1[:, :, :], start=True, stop=False)

            def proj_class(j):
                if j == 0:
                    pe.wait_ge(last_done, 1)
                pe.matmul(PROJ[j][:, :], last[:, :], ws1[:, :, :], start=False, stop=True).then_inc(proj_mm, 1)

            for j in range(J - 1):
                proj_hidden(j)
                proj_class(j)

            def transposes(j):
                pe.wait_ge(norm_act, j + 1)
                pe.wait_ge(norm_pool, j + 1)
                if j == 0:
                    pe.wait_ge(norm_vector, 1)
                if j == 2:
                    pe.wait_ge(ln_lo, 2)
                if j == 3:
                    pe.wait_ge(cwT_done, 1)
                for t in range(B):
                    done = pe.transpose(TR2[j][:, t * P:(t + 1) * P], xn[:, j % 2, t, :], ident[:, :])
                done.then_inc(ln_tr, 1)

            def gates(h):
                pe.wait_ge(ln_lo, GROUPS[h][1])
                if h == 1:
                    pe.wait_ge(gate_step, 1)
                    pe.wait_ge(cwT_done, 1)
                for n in range(B * (GROUPS[h][1] - GROUPS[h][0])):
                    j, to, tok = GROUPS[h][0] + n // B, GATE[:, n * E:(n + 1) * E], slice(n % B * P, (n % B + 1) * P)
                    pe.matmul(to, xh[:, j, tok], gw16[:, 0, :], start=True, stop=False)
                    pe.matmul(to, xl[:, j, tok], gw16[:, 0, :], start=False, stop=False)
                    done = pe.matmul(to, xh[:, j, tok], gw16[:, 1, :], start=False, stop=True)
                done.then_inc(gate_mm, 1)

            def weights_transposed(h):
                pe.wait_ge(gate_step, GSTEPS * (h + 1))
                for j in range(*GROUPS[h]):
                    done = pe.transpose(CWT[0:B * E, j * P:(j + 1) * P], cw[:, j * B:(j + 1) * B, :], ident[:, :])
                done.then_inc(cwT_mm, 1)

            def b3_term(j):
                if j == 0:
                    pe.wait_ge(b3_split, 2)
                    pe.wait_ge(ln_lo, J)
                    pe.wait_ge(cwT_done, 1)
                else:
                    pe.wait_ge(cwT_done, 2)
                    pe.wait_ge(b3_added, {1: 1, 2: 1, 3: 2}[j])
                for n, (c, b) in enumerate(((cwTh, b3h), (cwTh, b3l), (cwTl, b3h))):
                    done = pe.matmul(B3P[j][:, :], c[:, j, :], b[:, :, :], start=n == 0, stop=n == 2)
                done.then_inc(b3_mm, 1)

            transposes(0)
            proj_hidden(J - 1)
            meanwhile = {0: [(proj_class, 3)], 2: [(transposes, 1)], 5: [(transposes, 2), (weights_transposed, 0)],
                         6: [(transposes, 3)], 8: [(gates, 1)], 9: [(b3_term, 0)], 13: [(weights_transposed, 1)],
                         14: [(b3_term, 1), (b3_term, 2)], 15: [(b3_term, 3)]}

            def step(c, k):
                item = (c, k)
                i = place(c, k)
                if real(item):
                    layernormed = c + 1 if i is not None else J
                    if i == 0:
                        pe.wait_ge(wl_done, 1)
                    if k == 0:
                        pe.wait_ge(ln_hi, layernormed)
                    wait(pe, h1_done, at(item, -1))
                    z = Z1[k % 2][:, :]
                    pe.matmul(z, wh[:, 0, k, :], xh[:, c, :], start=True, stop=False)
                    pe.matmul(z, wl[:, 0, k, :], xh[:, c, :], start=False, stop=False)
                    if k == 0:
                        pe.wait_ge(ln_lo, layernormed)
                    pe.matmul(z, wh[:, 0, k, :], xl[:, c, :], start=False, stop=True).then_inc(z1_mm, 1)
                if i == 0:
                    gates(0)
                item = back(c, k, LAG2)
                if real(item):
                    e, q = item[1], item[1] % DEPTH
                    if i == LAG2:
                        pe.wait_ge(wl_done, 2)
                    if i in (LAG2, LAG2 + 1):
                        pe.wait_ge(ln_stat, e + 1)
                    wait(pe, r2_done, at(item, -1))
                    pe.wait_ge(h1_done, at(item))
                    z = Z2[e % 2][:, :]
                    pe.matmul(z, wh[:, 1, e, :], h1[:, q, :], start=True, stop=False)
                    pe.matmul(z, wl[:, 1, e, :], h1[:, q, :], start=False, stop=False)
                    pe.wait_ge(l1_done, at(item))
                    pe.matmul(z, wh[:, 1, e, :], l1[:, q, :], start=False, stop=True).then_inc(z2_mm, 1)
                item = back(c, k, LAG3)
                if real(item):
                    e, q = item[1], item[1] % DEPTH
                    wait(pe, y_used, at(item, -1))
                    if i == LAG3:
                        pe.wait_ge(wl_done, 3)
                    if i in (LAG3, LAG3 + 1):
                        pe.wait_ge(ln_stat, e + 3)
                    pe.wait_ge(h2_done, at(item))
                    for n, (h, w) in enumerate(((h2, wh), (h2, wl), (l2, wh))):
                        if n == 2:
                            wait_l2(pe, item)
                        for t in range(B):
                            done = pe.matmul(Y[e % 2][:, t * D:(t + 1) * D], h[:, q, t * P:(t + 1) * P], w[:, 2, e, :],
                                             start=(n, t) == (0, 0), stop=(n, t) == (2, B - 1), skip_group_check=True)
                    done.then_inc(y_mm, 1)
                for work, j in meanwhile.get(i, []):
                    work(j)

            over_items(pe, step, LAG3)


_INS = ["L0_attn_shot_embeddings", "L0_attn_Wd", "L0_attn_bd", "L0_attn_Wi", "L0_attn_bi", "L0_attn_A_log", "L0_attn_Wo",
        "L0_attn_bo", "L0_attn_Ws", "L0_attn_bs", "L0_ffn_gate_w", "L0_ffn_gate_b", "L0_ffn_w1", "L0_ffn_b1", "L0_ffn_w2",
        "L0_ffn_b2", "L0_ffn_w3", "L0_ffn_b3"]


def kernel(**inputs):
    import numpy as _np
    import concourse.bacc as _bacc
    from concourse.bass_utils import run_bass_kernel_spmd as _run

    nc = _bacc.Bacc("TRN2", target_bir_lowering=False, num_devices=1)
    arrays, args = {}, []
    for name in _INS:
        a = _np.ascontiguousarray(inputs[name])
        arrays[f"in_{name}"] = a
        args.append(nc.dram_tensor(f"in_{name}", a.shape, mybir.dt.from_np(a.dtype), kind="ExternalInput").ap())
    args.append(nc.dram_tensor("result", [B, S, D], F32, kind="ExternalOutput").ap())
    program(nc, *args)
    r = _run(nc, [arrays], core_ids=[0])
    return r.results[0]["result"]
```
